# Optimizing a Trainium2 kernel written in Bass

```python
import numpy as np
import jax
import jax.numpy as jnp

def _softmax(x, axis=-1):
    return jax.nn.softmax(x, axis=axis)

def _gelu(x):
    return jax.nn.gelu(x, approximate=True)

def _silu(x):
    return jax.nn.silu(x)

def _sigmoid(x):
    return jax.nn.sigmoid(x)

def _layernorm(x, axis=-1, eps=1e-05):
    m = jnp.mean(x, axis=axis, keepdims=True)
    v = jnp.var(x, axis=axis, keepdims=True)
    return (x - m) / jnp.sqrt(v + eps)

def _scatter_add(tgt, idx, src, axis=0):
    return tgt.at[idx].add(src)

def _segment_sum(src, seg, n):
    return jax.ops.segment_sum(src, seg, n)
kernel_name = 'mk_recurrent_d2_jaxref_r8_1ca995'

def setup_inputs(seed: int=0):
    np.random.seed(seed)
    _w = jnp.asarray

    def _L0_attn_setup():
        import jax, jax.numpy as jnp
        import numpy as np
        MAX_DISTANCE = 10
        BIAS_SCALE = 0.01

        def distance_bias(seq_len, dtype):
            pos = jnp.arange(seq_len, dtype=dtype)
            d = jnp.abs(pos[None, :] - pos[:, None])
            return jnp.clip(d, 0, MAX_DISTANCE) * BIAS_SCALE
        key = jax.random.key(seed)
        k1, k2 = jax.random.split(key)
        B, S, D_IN, D_OUT = (4, 256, 128, 128)
        x = jax.random.normal(k1, (B, S, D_IN), dtype=jnp.float32)
        W = jax.random.normal(k2, (D_OUT, D_IN), dtype=jnp.float32) * (1.0 / np.sqrt(D_IN))
        b = jnp.zeros((D_OUT,), dtype=jnp.float32)
        return {'x': x, 'W': W, 'b': b}
    _L0_attn_in = _L0_attn_setup()

    def _L0_ffn_setup():
        import jax, jax.numpy as jnp
        import numpy as np
        B, S, H = (2, 256, 128)
        E_ROUTED = 8
        TOP_K = 2
        I = 256
        key = jax.random.key(seed)
        ks = jax.random.split(key, 9)
        s = 0.02
        return {'x': jax.random.normal(ks[0], (B, S, H), dtype=jnp.float32), 'shared_gate': jax.random.normal(ks[1], (I, H), dtype=jnp.float32) * s, 'shared_up': jax.random.normal(ks[2], (I, H), dtype=jnp.float32) * s, 'shared_down': jax.random.normal(ks[3], (H, I), dtype=jnp.float32) * s, 'gate_w': jax.random.normal(ks[4], (E_ROUTED, H, I), dtype=jnp.float32) * s, 'up_w': jax.random.normal(ks[5], (E_ROUTED, H, I), dtype=jnp.float32) * s, 'down_w': jax.random.normal(ks[6], (E_ROUTED, I, H), dtype=jnp.float32) * s, 'router_w': jax.random.normal(ks[7], (E_ROUTED, H), dtype=jnp.float32) * s, 'routing_bias': jnp.zeros((E_ROUTED,), dtype=jnp.float32)}
    _L0_ffn_in = _L0_ffn_setup()

    def _L1_attn_setup():
        import jax, jax.numpy as jnp
        import numpy as np
        B, N, DIM, H = (8, 512, 128, 16)
        D = DIM // H
        EPS_NORM = 1e-12
        EPS_PI = 1e-08
        key = jax.random.key(seed)
        k1, k2, k3 = jax.random.split(key, 3)
        x = jax.random.normal(k1, (B, N, DIM), dtype=jnp.float32)
        Wqkv = jax.random.normal(k2, (DIM, DIM), dtype=jnp.float32) * (1.0 / np.sqrt(DIM))
        temp = jnp.ones((H, 1), dtype=jnp.float32)
        Wout = jax.random.normal(k3, (DIM, DIM), dtype=jnp.float32) * (1.0 / np.sqrt(DIM))
        bout = jnp.zeros((DIM,), dtype=jnp.float32)
        return {'x': x, 'Wqkv': Wqkv, 'temp': temp, 'Wout': Wout, 'bout': bout}
    _L1_attn_in = _L1_attn_setup()

    def _L1_ffn_setup():
        import jax, jax.numpy as jnp
        import numpy as np
        B, S, H = (8, 512, 128)
        NAV = 128
        E = 8
        F = 2 * H
        key = jax.random.key(seed)
        ks = jax.random.split(key, 12)

        def w(k, shape, fan_in):
            return jax.random.normal(k, shape, dtype=jnp.float32) / np.sqrt(fan_in)
        return {'hidden_states': jax.random.normal(ks[0], (B, S, H), dtype=jnp.float32), 'Wp1': w(ks[1], (H, NAV), H), 'bp1': jnp.zeros((NAV,), jnp.float32), 'Wp2': w(ks[2], (NAV, E), NAV), 'bp2': jnp.zeros((E,), jnp.float32), 'W1': w(ks[3], (E, H, F), H), 'b1': jnp.zeros((E, F), jnp.float32), 'W2': w(ks[4], (E, F, H), F), 'b2': jnp.zeros((E, H), jnp.float32), 'Wo': w(ks[5], (H, H), H), 'bo': jnp.zeros((H,), jnp.float32)}
    _L1_ffn_in = _L1_ffn_setup()
    _d = {'L0_attn_x': _L0_attn_in['x'], 'L0_attn_W': _L0_attn_in['W'], 'L0_attn_b': _L0_attn_in['b'], 'L0_ffn_shared_gate': _L0_ffn_in['shared_gate'], 'L0_ffn_shared_up': _L0_ffn_in['shared_up'], 'L0_ffn_shared_down': _L0_ffn_in['shared_down'], 'L0_ffn_gate_w': _L0_ffn_in['gate_w'], 'L0_ffn_up_w': _L0_ffn_in['up_w'], 'L0_ffn_down_w': _L0_ffn_in['down_w'], 'L0_ffn_router_w': _L0_ffn_in['router_w'], 'L0_ffn_routing_bias': _L0_ffn_in['routing_bias'], 'L1_attn_Wqkv': _L1_attn_in['Wqkv'], 'L1_attn_temp': _L1_attn_in['temp'], 'L1_attn_Wout': _L1_attn_in['Wout'], 'L1_attn_bout': _L1_attn_in['bout'], 'L1_ffn_Wp1': _L1_ffn_in['Wp1'], 'L1_ffn_bp1': _L1_ffn_in['bp1'], 'L1_ffn_Wp2': _L1_ffn_in['Wp2'], 'L1_ffn_bp2': _L1_ffn_in['bp2'], 'L1_ffn_W1': _L1_ffn_in['W1'], 'L1_ffn_b1': _L1_ffn_in['b1'], 'L1_ffn_W2': _L1_ffn_in['W2'], 'L1_ffn_b2': _L1_ffn_in['b2'], 'L1_ffn_Wo': _L1_ffn_in['Wo'], 'L1_ffn_bo': _L1_ffn_in['bo']}
    _x0 = _d['L0_attn_x']
    _d['L0_attn_x'] = jax.random.normal(jax.random.fold_in(jax.random.key(seed), 1), (16, 256, 128), dtype=_x0.dtype)
    del _x0
    return _d

def reference(L0_attn_x, L0_attn_W, L0_attn_b, L0_ffn_shared_gate, L0_ffn_shared_up, L0_ffn_shared_down, L0_ffn_gate_w, L0_ffn_up_w, L0_ffn_down_w, L0_ffn_router_w, L0_ffn_routing_bias, L1_attn_Wqkv, L1_attn_temp, L1_attn_Wout, L1_attn_bout, L1_ffn_Wp1, L1_ffn_bp1, L1_ffn_Wp2, L1_ffn_bp2, L1_ffn_W1, L1_ffn_b1, L1_ffn_W2, L1_ffn_b2, L1_ffn_Wo, L1_ffn_bo):

    def _L0_attn_ref(x, W, b):
        import jax, jax.numpy as jnp
        import numpy as np
        MAX_DISTANCE = 10
        BIAS_SCALE = 0.01

        def distance_bias(seq_len, dtype):
            pos = jnp.arange(seq_len, dtype=dtype)
            d = jnp.abs(pos[None, :] - pos[:, None])
            return jnp.clip(d, 0, MAX_DISTANCE) * BIAS_SCALE
        f = jnp.einsum('bsd,hd->bsh', x, W) + b
        e = jnp.einsum('bih,bjh->bij', f, f) + distance_bias(x.shape[1], f.dtype)[None]
        attn = jax.nn.softmax(e, axis=-1)
        a = jnp.einsum('bij,bjh->bih', attn, f)
        return a

    def _L0_ffn_ref(x, shared_gate, shared_up, shared_down, gate_w, up_w, down_w, router_w, routing_bias):
        import jax, jax.numpy as jnp
        import numpy as np
        B, S, H = (2, 256, 128)
        E_ROUTED = 8
        TOP_K = 2
        I = 256
        b, s, h = x.shape
        shared = jnp.einsum('bsi,hi->bsh', jax.nn.silu(jnp.einsum('bsh,ih->bsi', x, shared_gate)) * jnp.einsum('bsh,ih->bsi', x, shared_up), shared_down)
        logits = jnp.einsum('bsh,eh->bse', x, router_w) + routing_bias
        probs = jax.nn.sigmoid(logits)
        scores, indices = jax.lax.top_k(probs, TOP_K)
        scores = scores / jnp.sum(scores, axis=-1, keepdims=True)
        t = b * s
        xf = x.reshape(t, h)
        idx = indices.reshape(t, TOP_K)
        sc = scores.reshape(t, TOP_K)
        w = jnp.zeros((t, E_ROUTED), dtype=x.dtype)
        w = w.at[jnp.arange(t)[:, None], idx].add(sc)
        g = jax.nn.silu(jnp.einsum('th,ehi->tei', xf, gate_w))
        u = jnp.einsum('th,ehi->tei', xf, up_w)
        combined = jnp.einsum('tei,eih,te->th', g * u, down_w, w)
        return shared + combined.reshape(b, s, h)

    def _L1_attn_ref(x, Wqkv, temp, Wout, bout):
        import jax, jax.numpy as jnp
        import numpy as np
        B, N, DIM, H = (8, 512, 128, 16)
        D = DIM // H
        EPS_NORM = 1e-12
        EPS_PI = 1e-08
        b, n, dim = x.shape
        h, d = (H, dim // H)
        w = (x @ Wqkv.T).reshape(b, n, h, d).transpose(0, 2, 1, 3)
        norm = jnp.sqrt(jnp.sum(w * w, axis=-2, keepdims=True))
        w_normed = w / jnp.maximum(norm, EPS_NORM)
        logits = jnp.sum(w_normed * w_normed, axis=-1) * temp[None, :, :]
        Pi = jax.nn.softmax(logits, axis=1)
        Pi_norm = Pi / (jnp.sum(Pi, axis=-1, keepdims=True) + EPS_PI)
        dots = jnp.einsum('bhn,bhnd->bhd', Pi_norm, w * w)
        attn = 1.0 / (1.0 + dots)
        out = -(w * Pi[..., None]) * attn[:, :, None, :]
        out = out.transpose(0, 2, 1, 3).reshape(b, n, dim)
        return out @ Wout.T + bout

    def _L1_ffn_ref(hidden_states, Wp1, bp1, Wp2, bp2, W1, b1, W2, b2, Wo, bo):
        import jax, jax.numpy as jnp
        import numpy as np
        B, S, H = (8, 512, 128)
        NAV = 128
        E = 8
        F = 2 * H
        last = hidden_states[:, -1, :]
        logits = jax.nn.gelu(last @ Wp1 + bp1, approximate=False) @ Wp2 + bp2
        action_probs = jax.nn.softmax(logits, axis=-1)
        sel = jnp.argmax(action_probs, axis=-1)
        w1 = W1[sel]
        w2 = W2[sel]
        h = jax.nn.gelu(jnp.einsum('bsh,bhf->bsf', hidden_states, w1) + b1[sel][:, None, :], approximate=False)
        reasoned = jnp.einsum('bsf,bfh->bsh', h, w2) + b2[sel][:, None, :]
        out = reasoned @ Wo + bo
        return hidden_states + 0.3 * out
    x = L0_attn_x
    xn = _layernorm(x, axis=-1)
    s = _L0_attn_ref(xn, L0_attn_W, L0_attn_b)
    g = _silu(_L0_ffn_ref(xn, L0_ffn_shared_gate, L0_ffn_shared_up, L0_ffn_shared_down, L0_ffn_gate_w, L0_ffn_up_w, L0_ffn_down_w, L0_ffn_router_w, L0_ffn_routing_bias))
    x = x + s * g
    xn = _layernorm(x, axis=-1)
    s = _L1_attn_ref(xn, L1_attn_Wqkv, L1_attn_temp, L1_attn_Wout, L1_attn_bout)
    g = _silu(_L1_ffn_ref(xn, L1_ffn_Wp1, L1_ffn_bp1, L1_ffn_Wp2, L1_ffn_bp2, L1_ffn_W1, L1_ffn_b1, L1_ffn_W2, L1_ffn_b2, L1_ffn_Wo, L1_ffn_bo))
    x = x + s * g
    return x

_drawn_inputs = setup_inputs


def setup_inputs(seed=0):
    import zlib

    import numpy as np

    out = dict(_drawn_inputs(seed))
    spreads = {'L0_attn_b': (0.0, 0.8),
     'L0_ffn_routing_bias': (0.0, 0.8),
     'L1_attn_temp': (1.0, 0.6),
     'L1_attn_bout': (0.0, 0.1),
     'L1_ffn_bp1': (0.0, 0.1),
     'L1_ffn_bp2': (0.0, 0.1),
     'L1_ffn_b1': (0.0, 0.8),
     'L1_ffn_b2': (0.0, 0.8),
     'L1_ffn_bo': (0.0, 0.8)}
    factors = {'L0_attn_W': 8.0,
     'L0_ffn_shared_gate': 8.0,
     'L0_ffn_shared_up': 8.0,
     'L0_ffn_shared_down': 8.0,
     'L0_ffn_gate_w': 8.0,
     'L0_ffn_up_w': 8.0,
     'L0_ffn_down_w': 8.0,
     'L0_ffn_router_w': 8.0,
     'L1_attn_Wqkv': 2.972,
     'L1_attn_Wout': 2.988,
     'L1_ffn_Wp1': 4.757,
     'L1_ffn_Wp2': 4.536,
     'L1_ffn_W1': 4.586,
     'L1_ffn_W2': 4.152,
     'L1_ffn_Wo': 4.057}
    for name, (base, spread) in spreads.items():
        noise = np.random.default_rng([zlib.crc32(name.encode()), seed]).standard_normal(out[name].shape)
        drawn = base * np.exp(spread * noise) if base else spread * noise
        out[name] = jnp.asarray(drawn.astype(out[name].dtype))
    for name, factor in factors.items():
        out[name] = (out[name] * factor).astype(out[name].dtype)
    return out
```

```python
from contextlib import ExitStack

import numpy as np

import concourse.bass as bass
from concourse import mybir

F32 = mybir.dt.float32
BF16 = mybir.dt.bfloat16
I32 = mybir.dt.int32
U32 = mybir.dt.uint32
ALU = mybir.AluOpType
ACT = mybir.ActivationFunctionType
AX = mybir.AxisListType.X

NB = 16
NT = 32
NE = 8
NU = 71
NG = 18
ROW = 130
NOWHERE = 1 << 20
EPS = 1e-5

CW, _c = {}, 0
for _n, _w in [("ident", 128), ("dist", 512), ("upper", 128), ("e8", 256), ("unit", 72), ("head", 16)]:
    CW[_n] = (_c, _c + _w)
    _c += _w
CK = _c
AW, _c = {}, 0
for _n, _w in [("w0", 128), ("router", 8), ("rbias", 8), ("b0", 1)]:
    AW[_n] = (_c, _c + _w)
    _c += _w
AK = _c
DW, _c = {}, 0
for _n, _w in [("qkv", 128), ("wout", 128), ("wp1", 128), ("wp2", 8), ("bp1", 1), ("bp2", 8), ("temp", 16),
               ("bout", 128), ("wo", 128), ("bo", 128)]:
    DW[_n] = (_c, _c + _w)
    _c += _w
DK = _c
EK = 516


class Line:

    def __init__(self, sem):
        self.sem, self.count, self.steps, self.past = sem, 0, [], {}

    def wait(self, *toks):
        for t in toks:
            if t is None:
                continue
            if isinstance(t, list):
                self.wait(*t)
                continue
            sem, v = t
            if self.past.get(sem.name, 0) < v:
                self.past[sem.name] = v
                self.steps.append(lambda e, s=sem, n=v: e.wait_ge(s, n))

    def do(self, fn, *toks):
        self.wait(*toks)
        self.steps.append(fn)

    def tell(self, fn, *toks):
        self.wait(*toks)
        self.count += 1
        self.steps.append(lambda e, f=fn: f(e).then_inc(self.sem, 1))
        return (self.sem, self.count)

    def dma(self, fn, box, *toks):
        self.wait(*toks)
        box[1] += 16
        self.steps.append(lambda e, f=fn, s=box[0]: f(e).then_inc(s, 16))
        return (box[0], box[1])

    def run(self, e):
        for s in self.steps:
            s(e)


def mm(out, lhsT, rhs, start=True, stop=True):
    return lambda e: e.matmul(out, lhsT, rhs, start=start, stop=stop)


def tr(out, in_, ident):
    return lambda e: e.transpose(out, in_, ident)


def act(out, in_, func, bias=0.0, scale=1.0, accum=None):
    if accum is None:
        return lambda e: e.activation(out, in_, func, bias=bias, scale=scale)
    return lambda e: e.activation(out, in_, func, bias=bias, scale=scale, accum_out=accum)


def cp(out, in_):
    return lambda e: e.tensor_copy(out, in_)


def tt(out, a, b, op):
    return lambda e: e.tensor_tensor(out, a, b, op)


def ts(out, a, s1, s2=None, op0=ALU.mult, op1=None):
    if op1 is None:
        return lambda e: e.tensor_scalar(out, a, s1, None, op0)
    return lambda e: e.tensor_scalar(out, a, s1, s2, op0, op1)


def stt(out, a, s, b, op0, op1):
    return lambda e: e.scalar_tensor_tensor(out=out, in0=a, scalar=s, in1=b, op0=op0, op1=op1)


def ttr(out, a, b, op0, op1, init, accum):
    return lambda e: e.tensor_tensor_reduce(out, a, b, 1.0, init, op0, op1, accum)


def red(out, a, op, negate=False):
    if negate:
        return lambda e: e.tensor_reduce(out, a, AX, op, negate=True)
    return lambda e: e.tensor_reduce(out, a, AX, op)


def rcp(out, a):
    return lambda e: e.reciprocal(out, a)


def scan(out, a, b):
    return lambda e: e.tensor_tensor_scan(out, a, b, 0.0, ALU.mult, ALU.add)


def bc(ap, shape):
    return ap.unsqueeze(len(shape) - 1).broadcast_to(shape)


def program(nc, D, out):
    with ExitStack() as ctx:
        def sb(name, shape, dt=F32):
            return ctx.enter_context(nc.sbuf_tensor(name, shape, dt))

        def sem(name):
            return ctx.enter_context(nc.semaphore(name))

        X = sb("X", [128, NT, 128])
        XA = sb("XA", [128, NT, ROW])
        XB = sb("XB", [128, NT, ROW])
        XT = sb("XT", [128, NT * 128])
        FT = sb("FT", [128, NT * 128])
        F = sb("F", [128, NT, 128])
        S = sb("S", [128, NT, 128])
        SH = sb("SH", [128, NT, 128])
        C = sb("C", [128, CK])
        WA = sb("WA", [128, AK])
        WB = sb("WB", [128, 768])
        WE = sb("WE", [128, NE * 768])
        WD = sb("WD", [128, DK])
        DI = sb("DI", [128, 64], I32)
        E = sb("E", [128, 2, 2, 256])
        PR = sb("PR", [128, 2, 2, 256])
        PT = sb("PT", [128, 2, 2, 256])
        ST = sb("ST", [128, NT, 6])
        MV = sb("MV", [128, NT, 2])
        RS = sb("RS", [128, NT])
        NM = sb("NM", [128, NT])
        SU = sb("SU", [128, NT])
        EPSB = sb("EPSB", [128, 1])
        BFC = sb("BFC", [128, 3, 256], BF16)
        RW = sb("RW", [128, 12, 32])
        POS = sb("POS", [128, 2, NT], I32)
        NI = sb("NI", [128, 2, 8], I32)
        EU = sb("EU", [128, 72])
        EUI = sb("EUI", [128, 72], I32)
        ONE = sb("ONE", [128, 256])
        ZB = sb("ZB", [128, ROW])
        XS = sb("XS", [128, 4, 4, ROW])
        XG = sb("XG", [128, 2, 512])
        HT = sb("HT", [128, 3, 256])
        YS = sb("YS", [128, 8, 128])
        SG = FT[:, 0:1536].rearrange("p (a b) -> p a b", a=3)
        HH = FT[:, 1536:3072].rearrange("p (a b) -> p a b", a=3)
        xs_flat = XS[:, :, :, :].rearrange("p a b c -> p (a b c)")
        xg_flat = XG[:, :, :].rearrange("p a b -> p (a b)")
        R8 = xs_flat[:, 0:2048].rearrange("p (a b) -> p a b", a=8)
        WS = xs_flat[:, 0:4 * EK].rearrange("p (a b) -> p a b", a=4)
        UC = xg_flat[:, 0:504].rearrange("p (u e) -> p u e", e=7)
        JK = xg_flat[:, 0:256]
        PXP = YS[:, 0:4, :].rearrange("p (a b) d -> p a b d", a=2)
        OT = YS[:, 4:8, :].rearrange("p (a b) d -> p a (b d)", a=2)
        SM = sb("SM", [128, 8, 32])
        A1 = sb("A1", [128, 16])
        SEL = sb("SEL", [16, 6, 8])
        SELI = sb("SELI", [16, 8], U32)
        BO3 = sb("BO3", [128, 128])
        PS = [ctx.enter_context(nc.psum_tensor(f"PS{i}", [128, 512], F32)) for i in range(8)]

        xs = nc.dram_tensor("xs_scratch", [NG * 4 * 128, ROW], F32, kind="Internal").ap()
        yc = nc.dram_tensor("yc_scratch", [NB * 128 * 4, 128], F32, kind="Internal").ap()

        def c_(n):
            return C[:, CW[n][0]:CW[n][1]]

        def a_(n):
            return WA[:, AW[n][0]:AW[n][1]]

        def d_(n):
            return WD[:, DW[n][0]:DW[n][1]]

        ident = c_("ident")
        pe, dve, sc, po, sp = (Line(sem(n)) for n in ("pe", "dve", "act", "pool", "sp"))
        box = {}

        def dsem(name):
            if name not in box:
                box[name] = [sem("d_" + name), 0]
            return box[name]

        def load(dst, src, name, *toks):
            return sp.dma(lambda e: e.dma_start(dst, src), dsem(name), *toks)

        def tile(T, t, n=1):
            return T[:, t * 128:(t + n) * 128]

        free = [None] * 8

        x_in = []
        l_c = load(C[:, :], D["consts"], "c")
        l_wa = None
        for c in range(8):
            for b in (2 * c, 2 * c + 1):
                tok = load(X[:, 2 * b:2 * b + 2, :].rearrange("p i d -> p (i d)"),
                           D["x"][b].rearrange("(p i) d -> p (i d)", i=2), f"x{c}")
            x_in.append(tok)
            if c == 1:
                l_wa = load(WA[:, :], D["wa"], "wa")
        l_di = load(DI[:, :], D["dest"], "di")
        l_wb = load(WB[:, :], D["wb"], "wb")
        z1 = po.tell(lambda e: e.memset(ZB[:, :], 0.0))
        z2 = po.tell(lambda e: e.memset(ZB[:, 128:129].bitcast(I32), NOWHERE), z1)
        l_fill = load(xs.rearrange("(u p) r -> p u r", p=128), ZB[:, :].unsqueeze(1).broadcast_to([128, NG * 4, ROW]),
                      "fill", z2)
        l_we = load(WE[:, :], D["we"], "we")
        l_wd = load(WD[:, :], D["wd"], "wd")

        k_eps = po.tell(lambda e: e.memset(EPSB[:, :], EPS))
        k_one = po.tell(lambda e: e.memset(ONE[:, :], 1.0))
        k_bf1 = po.tell(lambda e: e.memset(BFC[:, 1, :], 1.0))

        def stats(T, t, *toks):
            a = dve.tell(lambda e: e.bn_stats(ST[:, t, :], T[:, t, :]), *toks)
            return dve.tell(lambda e: e.bn_aggr(MV[:, t, :], ST[:, t, :]), a)

        xt_done, xa_done, xb_done = [], [], []

        def norm_in(c):
            t0 = 4 * c
            for t in range(t0, t0 + 4):
                mv = stats(X, t, x_in[c])
            sd = sc.tell(act(RS[:, t0:t0 + 4], MV[:, t0:t0 + 4, 1], ACT.Sqrt, bias=EPSB[:, :]), mv, k_eps)
            rs = dve.tell(rcp(RS[:, t0:t0 + 4], RS[:, t0:t0 + 4]), sd)
            for t in range(t0, t0 + 4):
                xa = po.tell(ts(XA[:, t, 0:128], X[:, t, :], MV[:, t, 0:1], RS[:, t:t + 1], ALU.subtract, ALU.mult), rs)
            xa_done.append(xa)

        def turn_in(c):
            k = c % 2
            for j in range(4):
                tok = pe.tell(tr(PS[k][:, j * 128:(j + 1) * 128], XA[:, 4 * c + j, 0:128], ident), xa_done[c], l_c, free[k])
            free[k] = sc.tell(act(tile(XT, 4 * c, 4), PS[k][:, :], ACT.Copy), tok)
            xt_done.append(free[k])

        ft_done, f_done = [], []

        def logits(c):
            for t in range(4 * c, 4 * c + 4):
                tok = pe.tell(mm(PS[2][:, 8 * t:8 * t + 8], tile(XT, t), a_("router")), xt_done[c], l_wa)
            k = 3 + c % 2
            ft = pe.tell(mm(PS[k][:, :], a_("w0"), tile(XT, 4 * c, 4)), free[k])
            free[k] = sc.tell(act(tile(FT, 4 * c, 4), PS[k][:, :], ACT.Identity, bias=a_("b0")), ft, l_wa)
            ft_done.append(free[k])
            return tok

        def turn_f(c):
            k = 5 + c % 2
            for j in range(4):
                tok = pe.tell(tr(PS[k][:, j * 128:(j + 1) * 128], tile(FT, 4 * c + j), ident), ft_done[c], free[k])
            free[k] = dve.tell(cp(F[:, 4 * c:4 * c + 4, :], PS[k][:, :].rearrange("p (t d) -> p t d", d=128)), tok)
            f_done.append(free[k])

        for i in range(8 + 3):
            if i < 8:
                norm_in(i)
            if 1 <= i < 9:
                turn_in(i - 1)
            if 2 <= i < 10:
                lg = logits(i - 2)
            if 3 <= i:
                turn_f(i - 3)
        for c in range(8):
            xb_done.append(po.tell(cp(XB[:, 4 * c:4 * c + 4, 0:128], XA[:, 4 * c:4 * c + 4, 0:128]), xa_done[c]))

        def et(ap):
            return ap.rearrange("p (e t) -> p e t", e=NE)

        def te(ap):
            return ap.rearrange("p (e t) -> p t e", e=NE)

        def over_e(ap):
            return ap.unsqueeze(1).broadcast_to([128, NE, NT])

        lgs, prob, eq, cand, oh1, oh2, ex, pos = (R8[:, i, :] for i in range(8))
        m1, m2, i1, i2, rw, w1, w2 = (RW[:, i, :] for i in range(7))
        base = RW[:, 8:12, :].rearrange("p a b -> p (a b)")
        n_e, pad, cum, corr = (base[:, 8 * i:8 * i + 8] for i in range(4))

        upper = dve.tell(cp(BFC[:, 0, 0:128], c_("upper")), l_c)
        q = dve.tell(tt(et(lgs), PS[2][:, 0:256].rearrange("p (t e) -> p e t", e=NE), bc(a_("rbias"), [128, NE, NT]),
                        ALU.add), lg, l_wa)
        free[2] = q
        q = sc.tell(act(prob, lgs, ACT.Sigmoid), q)

        def top(p, m, i, oh, tok):
            tok = dve.tell(red(m, te(p), ALU.max), tok)
            tok = dve.tell(tt(et(eq), et(p), over_e(m), ALU.is_equal), tok)
            tok = dve.tell(tt(cand, eq, c_("e8"), ALU.mult), tok)
            tok = dve.tell(red(i, te(cand), ALU.min), tok)
            return dve.tell(tt(et(oh), et(c_("e8")), over_e(i), ALU.is_equal), tok)

        q = top(prob, m1, i1, oh1, q)
        q = dve.tell(stt(lgs, oh1, -2.0, prob, ALU.mult, ALU.add), q)
        q = top(lgs, m2, i2, oh2, q)
        mask = dve.tell(tt(BFC[:, 2, :], oh1, oh2, ALU.add), q)
        r1 = pe.tell(mm(PS[7][:, 0:256], BFC[:, 0, 0:128], BFC[:, 2, :]), mask, upper, free[7])
        r2 = pe.tell(mm(PS[7][:, 256:512], BFC[:, 1, 0:128], BFC[:, 2, :]), k_bf1)
        within, total = PS[7][:, 0:256], PS[7][:, 256:512]
        w = dve.tell(tt(rw, m1, m2, ALU.add))
        w = dve.tell(rcp(rw, rw), w)
        dve.do(tt(XA[:, :, 129], m1, rw, ALU.mult), w, *xa_done)
        dve.do(tt(XB[:, :, 129], m2, rw, ALU.mult))
        dve.do(cp(XA[:, :, 128].bitcast(I32), DI[:, 0:32]), l_di)
        cols = dve.tell(cp(XB[:, :, 128].bitcast(I32), DI[:, 32:64]))
        q = dve.tell(scan(cand, ONE[:, :], total), r2, k_one)
        q = dve.tell(tt(ex, cand, total, ALU.subtract), q)
        q = dve.tell(tt(n_e, et(cand)[:, :, 31], et(ex)[:, :, 0], ALU.subtract), q)
        q = dve.tell(ts(NI[:, 0, :], n_e, 127.0, None, ALU.add), q)
        q = dve.tell(ts(NI[:, 1, :], NI[:, 0, :], -128, None, ALU.bitwise_and), q)
        q = dve.tell(cp(pad, NI[:, 1, :]), q)
        cq = dve.tell(scan(cum, ONE[:, 0:8], pad), q)
        q = dve.tell(tt(corr, cum, pad, ALU.subtract), cq)
        q = dve.tell(tt(corr, corr, et(ex)[:, :, 0], ALU.subtract), q)
        free[7] = dve.tell(tt(pos, within, ex, ALU.add), q)
        q = dve.tell(tt(et(pos), et(pos), bc(corr, [128, NE, NT]), ALU.add), free[7])
        q1 = dve.tell(tt(oh1, oh1, pos, ALU.mult), q)
        q2 = dve.tell(tt(oh2, oh2, pos, ALU.mult), q)
        dve.do(red(w1, te(oh1), ALU.add), q1)
        q = dve.tell(red(w2, te(oh2), ALU.add), q2)
        places = dve.tell(cp(POS[:, :, :], RW[:, 5:7, :]), q)
        q = dve.tell(tt(UC[:, :, :], bc(c_("unit"), [128, 72, 7]), cum[:, 0:7].unsqueeze(1).broadcast_to([128, 72, 7]),
                        ALU.is_ge), cq)
        q = dve.tell(red(EU[:, :], UC[:, :, :], ALU.add), q)
        experts = dve.tell(ts(EUI[:, :], EU[:, :], 768.0, None, ALU.mult), q)

        def scatter(dst, idx, src, name, bound, *toks):
            return po.dma(lambda e: e.indirect_dma_start(
                out=dst, out_offset=bass.IndirectOffsetOnAxis(ap=idx, axis=0), in_=src, in_offset=None,
                bounds_check=bound, oob_is_err=False), dsem(name), *toks)

        po.wait(places, cols, l_fill, *xb_done)
        for t in range(NT):
            scatter(xs, POS[:, 0, t:t + 1], XA[:, t, :], "disp", NG * 4 * 128 - 1)
            dispatched = scatter(xs, POS[:, 1, t:t + 1], XB[:, t, :], "disp", NG * 4 * 128 - 1)

        sc_done, ex_done, pt_done = {}, {}, {}
        pv_read, s_done = {}, {}

        def scores(b):
            k = b % 2
            for i in range(2):
                tok = pe.tell(mm(PS[k][:, i * 256:(i + 1) * 256], tile(FT, 2 * b + i), tile(FT, 2 * b, 2)),
                              ft_done[b // 2], free[k])
            for i in range(2):
                t = 2 * b + i
                e1 = dve.tell(ttr(E[:, k, i, :], PS[k][:, i * 256:(i + 1) * 256],
                                  c_("dist")[:, i * 256:(i + 1) * 256], ALU.add, ALU.max, -3.0e38, RW[:, 7, t:t + 1]),
                              tok, l_c, ex_done.get(b - 2))
            free[k] = e1
            nm = dve.tell(ts(NM[:, 2 * b:2 * b + 2], RW[:, 7, 2 * b:2 * b + 2], -1.0), e1)
            for i in range(2):
                t = 2 * b + i
                tok = sc.tell(act(PR[:, k, i, :], E[:, k, i, :], ACT.Exp, bias=NM[:, t:t + 1], accum=SU[:, t:t + 1]),
                              nm, pt_done.get(b - 2))
            ex_done[b] = tok
            sc_done[b] = dve.tell(rcp(SU[:, 2 * b:2 * b + 2], SU[:, 2 * b:2 * b + 2]), tok)

        def turn_p(b):
            k, kb = 3 + b % 2, b % 2
            for j in range(2):
                for i in range(2):
                    tok = pe.tell(tr(PS[k][:, j * 256 + i * 128:j * 256 + (i + 1) * 128],
                                     PR[:, kb, i, j * 128:(j + 1) * 128], ident), ex_done[b], free[k])
            pt_done[b] = tok
            free[k] = dve.tell(cp(PT[:, kb, :, :], PS[k][:, :].rearrange("p (j i) -> p j i", j=2)), tok, pv_read.get(b - 2))

        def mix(b):
            k, kb = 5 + b % 2, b % 2
            for i in range(2):
                for j in range(2):
                    tok = pe.tell(mm(PS[k][:, i * 128:(i + 1) * 128], PT[:, kb, j, i * 128:(i + 1) * 128],
                                     F[:, 2 * b + j, :], start=j == 0, stop=j == 1),
                                  free[3 + b % 2], free[k], f_done[b // 2])
            pv_read[b] = tok
            for i in range(2):
                t = 2 * b + i
                free[k] = sc.tell(act(S[:, t, :], PS[k][:, i * 128:(i + 1) * 128], ACT.Copy, scale=SU[:, t:t + 1]),
                                  tok, sc_done[b])
            s_done[b] = free[k]

        for i in range(NB + 2):
            if i < NB:
                scores(i)
            if 1 <= i < NB + 1:
                turn_p(i - 1)
            if i >= 2:
                mix(i - 2)

        h_done, h_read, sg_read = {}, {}, {}

        def up(j):
            c, f = divmod(j, 2)
            k = 2 * (j % 2)
            g = pe.tell(mm(PS[k][:, :], WB[:, f * 128:(f + 1) * 128], tile(XT, 4 * c, 4)), l_wb, free[k])
            u = pe.tell(mm(PS[k + 1][:, :], WB[:, 256 + f * 128:256 + (f + 1) * 128], tile(XT, 4 * c, 4)), free[k + 1])
            free[k] = sc.tell(act(SG[:, j % 3, :], PS[k][:, :], ACT.Silu), g, sg_read.get(j - 3), sc_done[NB - 1])
            free[k + 1] = dve.tell(tt(HH[:, j % 3, :], SG[:, j % 3, :], PS[k + 1][:, :], ALU.mult), u, free[k],
                                   h_read.get(j - 3))
            sg_read[j] = h_done[j] = free[k + 1]

        def down(c):
            k = 4 + c % 2
            for t in range(4):
                for f in range(2):
                    tok = pe.tell(mm(PS[k][:, t * 128:(t + 1) * 128], HH[:, (2 * c + f) % 3, t * 128:(t + 1) * 128],
                                     WB[:, 512 + f * 128:512 + (f + 1) * 128], start=f == 0, stop=f == 1),
                                  h_done[2 * c + 1], free[k])
            h_read[2 * c] = h_read[2 * c + 1] = tok
            free[k] = sc.tell(act(SH[:, 4 * c:4 * c + 4, :], PS[k][:, :].rearrange("p (t d) -> p t d", d=128), ACT.Copy), tok)
            return free[k]

        for j in range(16):
            up(j)
            if j % 2 == 0 and j:
                down(j // 2 - 1)
        sh_done = down(7)

        xs_in, xs_read, xg_done, xg_read = {}, {}, {}, {}
        gu_done, eh_done, ehr, ht_done, ht_read, y_out = {}, {}, {}, {}, {}, {}
        ys_done = {}
        nu = [min(4, NU - 4 * g) for g in range(NG)]

        def fetch(g):
            n = nu[g]
            xs_in[g] = load(XS[:, g % 4, 0:n, :], xs[g * 512:g * 512 + n * 128, :].rearrange("(u p) r -> p u r", p=128),
                            f"xs{g % 4}", dispatched, xs_read.get(g - 4), y_out.get(4 * (g - 4) + 3))

        def turn_x(g):
            for j in range(nu[g]):
                tok = pe.tell(tr(PS[6][:, j * 128:(j + 1) * 128], XS[:, g % 4, j, 0:128], ident), xs_in[g], free[6])
            xs_read[g] = tok
            free[6] = sc.tell(act(XG[:, g % 2, 0:nu[g] * 128], PS[6][:, 0:nu[g] * 128], ACT.Copy), tok, xg_read.get(g - 2))
            xg_done[g] = free[6]

        reg = {}

        def pick(u):
            def f(e):
                reg[u] = e.value_load(EUI[0:1, u:u + 1], min_val=0, max_val=7 * 768)
            pe.do(f, experts, l_we)

        def gate_up(u):
            g, j = divmod(u, 4)
            k = u % 3
            pick(u)
            tok = pe.tell(lambda e: e.matmul(PS[k][:, :], XG[:, g % 2, j * 128:(j + 1) * 128], WE[:, bass.ds(reg[u], 512)],
                                             start=True, stop=True), xg_done[g], free[k])
            if j == nu[g] - 1:
                xg_read[g] = tok
            a = sc.tell(act(SG[:, u % 3, 0:256], PS[k][:, 0:256], ACT.Silu), tok, sg_read.get(("e", u - 3)), sg_read[15])
            free[k] = dve.tell(tt(HH[:, u % 3, 0:256], SG[:, u % 3, 0:256], PS[k][:, 256:512], ALU.mult), a,
                               ehr.get(u - 3), h_read[15])
            sg_read[("e", u)] = eh_done[u] = free[k]

        def turn_h(u):
            k = 3 + u % 2
            for f in range(2):
                tok = pe.tell(tr(PS[k][:, f * 128:(f + 1) * 128], HH[:, u % 3, f * 128:(f + 1) * 128], ident),
                              eh_done[u], free[k])
            ehr[u] = tok
            free[k] = dve.tell(cp(HT[:, u % 3, :], PS[k][:, 0:256]), tok, ht_read.get(u - 3))
            ht_done[u] = free[k]

        def down_e(u):
            g, j = divmod(u, 4)
            k = (5, 7)[u % 2]
            for f in range(2):
                tok = pe.tell(lambda e, f=f: e.matmul(PS[k][:, 0:128], HT[:, u % 3, f * 128:(f + 1) * 128],
                                                      WE[:, bass.ds(reg[u] + (512 + f * 128), 128)],
                                                      start=f == 0, stop=f == 1), ht_done[u], free[k])
            ht_read[u] = tok
            free[k] = sc.tell(act(YS[:, u % 8, :], PS[k][:, 0:128], ACT.Copy, scale=XS[:, g % 4, j, 129:130]), tok,
                              y_out.get(u - 8))
            ys_done[u] = free[k]
            y_out[u] = scatter(yc, XS[:, g % 4, j, 128:129].bitcast(U32), YS[:, u % 8, :], f"y{u % 8}", NB * 128 * 4 - 1,
                               ys_done[u])

        for g in range(3):
            fetch(g)
        turn_x(0)
        for u in range(NU + 3):
            if u < NU:
                gate_up(u)
                if u % 4 == 2 and u // 4 + 1 < NG:
                    turn_x(u // 4 + 1)
                if u % 4 == 3 and u // 4 + 3 < NG:
                    fetch(u // 4 + 3)
            if 2 <= u < NU + 2:
                turn_h(u - 2)
            if u >= 3:
                down_e(u - 3)
        routed = [y_out[u] for u in range(NU - 8, NU)]

        YT = FT
        yt_read, x1_mid = {}, {}
        x1_done, xn_done, xt1_done = {}, {}, {}
        bo3 = dve.tell(ts(BO3[:, :], d_("bo"), 0.3), l_wd)

        def two(T, b, w=128):
            return T[:, 2 * b:2 * b + 2, 0:w]

        def end0(b):
            s = b % 8
            yin = load(YT[:, s * 512:(s + 1) * 512], yc.rearrange("(b p q) d -> b p (q d)", b=NB, q=4)[b], f"yt{s}",
                       *routed, yt_read.get(b - 8), ft_done[7], sc_done[NB - 1])
            y4 = YT[:, s * 512:(s + 1) * 512].rearrange("p (i s d) -> p i s d", i=2, s=2)
            a = po.tell(tt(two(F, b), y4[:, :, 0, :], y4[:, :, 1, :], ALU.add), yin, pv_read[NB - 1])
            yt_read[b] = a
            t = dve.tell(tt(two(SH, b), two(SH, b), two(F, b), ALU.add), a, sh_done)
            g = sc.tell(act(two(F, b), two(SH, b), ACT.Silu), t)
            m = po.tell(tt(two(F, b), two(F, b), two(S, b), ALU.mult), g, s_done[b])
            x1_done[b] = dve.tell(tt(two(X, b), two(X, b), two(F, b), ALU.add), m)
            for i in range(2):
                x1_mid[b] = stats(X, 2 * b + i, x1_done[b])

        def norm1(bs):
            t0, t1 = 2 * bs[0], 2 * bs[-1] + 2
            sd = sc.tell(act(RS[:, t0:t1], MV[:, t0:t1, 1], ACT.Sqrt, bias=EPSB[:, :]), x1_mid[bs[-1]])
            rs = dve.tell(rcp(RS[:, t0:t1], RS[:, t0:t1]), sd)
            for b in bs:
                for t in (2 * b, 2 * b + 1):
                    tok = dve.tell(ts(XA[:, t, 0:128], X[:, t, :], MV[:, t, 0:1], RS[:, t:t + 1], ALU.subtract, ALU.mult), rs)
                xn_done[b] = tok
            for b in bs:
                k = b % 2
                for i in range(2):
                    tok = pe.tell(tr(PS[k][:, i * 128:(i + 1) * 128], XA[:, 2 * b + i, 0:128], ident), xn_done[b], free[k])
                free[k] = sc.tell(act(tile(XT, 2 * b, 2), PS[k][:, 0:256], ACT.Copy), tok)
                xt1_done[b] = free[k]

        for g in range(4):
            for b in range(4 * g, 4 * g + 4):
                end0(b)
            norm1(list(range(4 * g, 4 * g + 4)))

        tok = pe.tell(mm(PS[7][:, 0:16], d_("wp1"), XT[:, 255::256]), l_wd, xt1_done[15], free[7])
        tok = sc.tell(act(A1[:, :], PS[7][:, 0:16], ACT.Gelu, bias=d_("bp1")), tok)
        tok = pe.tell(mm(PS[7][0:16, 0:8], A1[:, :], d_("wp2")), tok)
        lt = SEL[:, 0, :]
        tok = dve.tell(tt(lt, PS[7][0:16, 0:8], d_("bp2")[0:16, :], ALU.add), tok)
        free[7] = tok
        tok = dve.tell(red(SEL[:, 1, 0:1], lt, ALU.max, negate=True), tok)
        tok = sc.tell(act(SEL[:, 2, :], lt, ACT.Exp, bias=SEL[:, 1, 0:1], accum=SEL[:, 3, 0:1]), tok)
        tok = dve.tell(rcp(SEL[:, 3, 0:1], SEL[:, 3, 0:1]), tok)
        tok = dve.tell(ts(SEL[:, 2, :], SEL[:, 2, :], SEL[:, 3, 0:1]), tok)
        tok = dve.tell(lambda e: e.max(SEL[:, 4, :], SEL[:, 2, :]), tok)
        chosen = dve.tell(lambda e: e.max_index(SELI[:, :], SEL[:, 4, :], SEL[:, 2, :]), tok)
        ws_in, ws_read = {}, {}

        def expert1(b):
            s = b % 4

            def f(e):
                v = e.value_load(SELI[b:b + 1, 0:1], min_val=0, max_val=7)
                return e.dma_start(WS[:, s, :], D["w1"][bass.ds(v, 1)].rearrange("o p k -> p (o k)"))
            ws_in[b] = sp.dma(f, dsem(f"ws{s}"), chosen, routed, ws_read.get(b - 4))

        for b in range(4):
            expert1(b)

        WT, W2, PX = FT, XB, PR
        N2, RN, DOT, SPI = (SM[:, i, 0:16] for i in range(4))
        HM = SM[:, 4, 0:16]
        HB = sb("HB", [128, 2, 16])
        LG = sb("LG", [128, 2, 2, 16])
        MX = sb("MX", [128, 2, 4])
        XNB = SH
        hm = dve.tell(tt(HM, c_("head"), d_("temp"), ALU.mult), l_wd, l_c)
        w_done, hb_done, hb_read, lg_done, px_done, px_read, ot_done, ot_read, s1_done = ({} for _ in range(9))

        def w2v(b):
            return W2[:, 2 * b:2 * b + 2, 0:128]

        def proj(b):
            k = b % 2
            tok = pe.tell(mm(PS[k][:, 0:256], d_("qkv"), tile(XT, 2 * b, 2)), xt1_done[b], l_wd, free[k])
            n2 = sc.tell(act(w2v(b), PS[k][:, 0:256].rearrange("p (i d) -> p i d", i=2), ACT.Square, accum=N2[:, b:b + 1]),
                         tok, dispatched)
            free[k] = sc.tell(act(tile(WT, 2 * b, 2), PS[k][:, 0:256], ACT.Copy), yt_read[15])
            w_done[b] = free[k]
            r = dve.tell(ts(RN[:, b:b + 1], N2[:, b:b + 1], 1e-24, None, ALU.max), n2)
            r = dve.tell(rcp(RN[:, b:b + 1], RN[:, b:b + 1]), r)
            hb_done[b] = dve.tell(ts(HB[:, b % 2, :], HM, RN[:, b:b + 1]), r, hm, hb_read.get(b - 2))

        def heads(b):
            k, s = 2 + b % 2, b % 2
            for i in range(2):
                tok = pe.tell(mm(PS[k][:, i * 16:(i + 1) * 16], W2[:, 2 * b + i, 0:128], HB[:, s, :]), hb_done[b], free[k])
            hb_read[b] = tok
            lg = PS[k][:, 0:32].rearrange("p (i h) -> p i h", i=2)
            m = dve.tell(red(MX[:, s, 0:2], lg, ALU.max), tok)
            free[k] = dve.tell(tt(LG[:, s, :, :], lg, bc(MX[:, s, 0:2], [128, 2, 16]), ALU.subtract), m)
            x = sc.tell(act(LG[:, s, :, :], LG[:, s, :, :], ACT.Exp), free[k])
            m = dve.tell(red(MX[:, s, 2:4], LG[:, s, :, :], ALU.add), x)
            m = dve.tell(rcp(MX[:, s, 2:4], MX[:, s, 2:4]), m)
            px_done[b] = dve.tell(tt(PXP[:, s, :, :].rearrange("p i (h d) -> p i h d", d=8),
                                     bc(LG[:, s, :, :], [128, 2, 16, 8]),
                                     MX[:, s, 2:4].unsqueeze(2).unsqueeze(3).broadcast_to([128, 2, 16, 8]), ALU.mult),
                                  m, px_read.get(b - 2))

        def spread(b):
            k, s, ks = 4 + b % 2, b % 2, 6
            for i in range(2):
                tok = pe.tell(tr(PS[k][:, i * 128:(i + 1) * 128], PXP[:, s, i, :], ident), px_done[b], free[k])
            for i in range(2):
                t2 = pe.tell(mm(PS[ks][:, 0:1], PXP[:, s, i, :], ONE[:, 0:1], start=i == 0, stop=i == 1), free[ks])
            px_read[b] = t2
            q = dve.tell(ts(SPI[:, b:b + 1], PS[ks][:, 0:1], 1e-8, None, ALU.add), t2)
            free[ks] = q
            q = dve.tell(rcp(SPI[:, b:b + 1], SPI[:, b:b + 1]), q)
            d = dve.tell(ttr(JK.rearrange("p (i d) -> p i d", i=2),
                             PS[k][:, 0:256].rearrange("p (i d) -> p i d", i=2), w2v(b), ALU.mult, ALU.add, 0.0,
                             DOT[:, b:b + 1]), tok)
            q = dve.tell(ts(DOT[:, b:b + 1], DOT[:, b:b + 1], SPI[:, b:b + 1], 1.0, ALU.mult, ALU.add), d, q)
            q = dve.tell(rcp(DOT[:, b:b + 1], DOT[:, b:b + 1]), q)
            free[k] = dve.tell(stt(OT[:, s, :], PS[k][:, 0:256], DOT[:, b:b + 1], tile(WT, 2 * b, 2), ALU.mult, ALU.mult),
                               q, w_done[b], ot_read.get(b - 2))
            ot_done[b] = free[k]

        def out1(b):
            k, s = 7, b % 2
            for i in range(2):
                tok = pe.tell(mm(PS[k][:, i * 128:(i + 1) * 128], OT[:, s, i * 128:(i + 1) * 128], d_("wout")),
                              ot_done[b], free[k])
            ot_read[b] = tok
            free[k] = dve.tell(tt(two(S, b), d_("bout").unsqueeze(1).broadcast_to([128, 2, 128]),
                                  PS[k][:, 0:256].rearrange("p (i d) -> p i d", i=2), ALU.subtract), tok)
            s1_done[b] = free[k]

        for i in range(NB + 3):
            if i < NB:
                proj(i)
            if 1 <= i < NB + 1:
                heads(i - 1)
            if 2 <= i < NB + 2:
                spread(i - 2)
            if i >= 3:
                out1(i - 3)

        H1 = E
        RT = PT
        xnb_done, h1_done, h1_read, rt_done, rt_read, t_done = {}, {}, {}, {}, {}, {}
        for b in range(NB):
            xnb_done[b] = po.tell(tt(two(XNB, b), two(XA, b), BO3[:, :].unsqueeze(1).broadcast_to([128, 2, 128]), ALU.add),
                                  xn_done[b], bo3)

        def ff_up(b):
            k, s = b % 2, b % 4
            for f in range(2):
                tok = pe.tell(mm(PS[k][:, f * 256:(f + 1) * 256], WS[:, s, f * 128:(f + 1) * 128], tile(XT, 2 * b, 2)),
                              ws_in[b], free[k])
            for f in range(2):
                free[k] = sc.tell(act(H1[:, b % 2, f, :], PS[k][:, f * 256:(f + 1) * 256], ACT.Gelu,
                                      bias=WS[:, s, 512 + f:513 + f]), tok, h1_read.get(b - 2))
            h1_done[b] = free[k]

        def ff_down(b):
            k, s = 2 + b % 2, b % 4
            for f in range(2):
                tok = pe.tell(mm(PS[k][:, 0:256], WS[:, s, 256 + f * 128:256 + (f + 1) * 128], H1[:, b % 2, f, :],
                                 start=f == 0, stop=f == 1), h1_done[b], free[k])
            h1_read[b] = tok
            free[k] = dve.tell(ts(RT[:, b % 2, 0, :], PS[k][:, 0:256], WS[:, s, 514:515], None, ALU.add), tok,
                               rt_read.get(b - 2))
            rt_done[b] = ws_read[b] = free[k]
            if b + 4 < NB:
                expert1(b + 4)

        def ff_out(b):
            k = 4 + b % 2
            for i in range(2):
                tok = pe.tell(mm(PS[k][:, i * 128:(i + 1) * 128], RT[:, b % 2, 0, i * 128:(i + 1) * 128], d_("wo")),
                              rt_done[b], free[k])
            rt_read[b] = tok
            free[k] = dve.tell(stt(two(XNB, b), PS[k][:, 0:256].rearrange("p (i d) -> p i d", i=2), 0.3, two(XNB, b),
                                   ALU.mult, ALU.add), tok, xnb_done[b])
            t_done[b] = free[k]

        def end1(b):
            g = sc.tell(act(two(F, b), two(XNB, b), ACT.Silu), t_done[b])
            m = po.tell(tt(two(F, b), two(F, b), two(S, b), ALU.mult), g, s1_done[b])
            a = dve.tell(tt(two(X, b), two(X, b), two(F, b), ALU.add), m)
            return load(out[b].rearrange("(p i) d -> p (i d)", i=2), two(X, b).rearrange("p i d -> p (i d)"), "out", a)

        for i in range(NB + 2):
            if i < NB:
                ff_up(i)
            if 1 <= i < NB + 1:
                ff_down(i - 1)
            if i >= 2:
                ff_out(i - 2)
                if (i - 2) % 4 == 3:
                    for b in range(i - 5, i - 1):
                        stored = end1(b)
        sp.wait(stored, dispatched, l_fill, *[y_out[u] for u in range(NU)])

        block = ctx.enter_context(nc.Block())

        @block.sync
        def _(e):
            sp.run(e)

        @block.tensor
        def _(e):
            pe.run(e)

        @block.vector
        def _(e):
            dve.run(e)

        @block.scalar
        def _(e):
            sc.run(e)

        @block.gpsimd
        def _(e):
            po.run(e)


def constants():
    p = np.arange(128)
    c = np.zeros((128, CK), np.float32)

    def put(name, a):
        c[:, CW[name][0]:CW[name][1]] = a
    put("ident", np.eye(128, dtype=np.float32))
    i = 2 * p[:, None, None, None] + np.arange(2)[None, :, None, None]
    j = 2 * p[None, None, None, :] + np.arange(2)[None, None, :, None]
    put("dist", (np.clip(np.abs(i - j), 0, 10).astype(np.float32) * np.float32(0.01)).reshape(128, 512))
    put("upper", (p[:, None] < p[None, :]).astype(np.float32))
    put("e8", np.repeat(np.arange(8) - 8, 32).astype(np.float32)[None, :])
    put("unit", (128 * np.arange(72)).astype(np.float32)[None, :])
    put("head", (p[:, None] // 8 == np.arange(16)[None, :]).astype(np.float32))
    t = np.arange(NT)
    slot0 = ((t[None, :] // 2 * 128 + p[:, None]) * 4 + 2 * (t[None, :] % 2)).astype(np.int32)
    return c, np.concatenate([slot0, slot0 + 1], axis=1).astype(np.int32)


def layout(a):
    def rep(v):
        return np.broadcast_to(v.reshape(1, -1), (128, v.size))

    def halves(m):
        return np.concatenate([m[0:128], m[128:256]], axis=1)

    consts, dest = constants()
    wa = np.concatenate([a["L0_attn_W"].T, a["L0_ffn_router_w"].T, rep(a["L0_ffn_routing_bias"]),
                         a["L0_attn_b"].reshape(128, 1)], axis=1)
    wb = np.concatenate([a["L0_ffn_shared_gate"].T, a["L0_ffn_shared_up"].T, halves(a["L0_ffn_shared_down"].T)], axis=1)
    we = np.concatenate([np.concatenate([a["L0_ffn_gate_w"][e], a["L0_ffn_up_w"][e], halves(a["L0_ffn_down_w"][e])], axis=1)
                         for e in range(8)], axis=1)
    temp = a["L1_attn_temp"].reshape(16)
    wd = np.concatenate([a["L1_attn_Wqkv"].T, a["L1_attn_Wout"].T, a["L1_ffn_Wp1"], a["L1_ffn_Wp2"],
                         a["L1_ffn_bp1"].reshape(128, 1), rep(a["L1_ffn_bp2"]), rep(temp), rep(a["L1_attn_bout"]),
                         a["L1_ffn_Wo"], rep(a["L1_ffn_bo"])], axis=1)
    w1 = np.stack([np.concatenate([a["L1_ffn_W1"][e], halves(a["L1_ffn_W2"][e]), a["L1_ffn_b1"][e].reshape(2, 128).T,
                                   a["L1_ffn_b2"][e].reshape(128, 1), np.zeros((128, 1), np.float32)], axis=1)
                   for e in range(8)])
    return {"x": a["L0_attn_x"], "consts": consts, "dest": dest, "wa": wa, "wb": wb, "we": we, "wd": wd, "w1": w1}


def kernel(**inputs):
    import concourse.bacc as bacc
    from concourse.bass_utils import run_bass_kernel_spmd as run

    nc = bacc.Bacc("TRN2", target_bir_lowering=False, num_devices=1)
    arrays = {n: np.ascontiguousarray(v) for n, v in layout({k: np.asarray(v) for k, v in inputs.items()}).items()}
    aps = {n: nc.dram_tensor(f"in_{n}", v.shape, mybir.dt.from_np(v.dtype), kind="ExternalInput").ap()
           for n, v in arrays.items()}
    out = nc.dram_tensor("out_0", (16, 256, 128), F32, kind="ExternalOutput").ap()
    program(nc, aps, out)
    r = run(nc, [{f"in_{n}": v for n, v in arrays.items()}], core_ids=[0])
    return r.results[0]["out_0"]
```

```python
from contextlib import ExitStack

import numpy as np

import concourse.bass as bass
from concourse import mybir

F32 = mybir.dt.float32
BF16 = mybir.dt.bfloat16
I32 = mybir.dt.int32
U32 = mybir.dt.uint32
ALU = mybir.AluOpType
ACT = mybir.ActivationFunctionType
AX = mybir.AxisListType.X

NB = 16
NT = 32
NE = 8
NU = 71
NG = 18
ROW = 130
NOWHERE = 1 << 20
EPS = 1e-5

CW, _c = {}, 0
for _n, _w in [("ident", 128), ("dist", 512), ("upper", 128), ("e8", 256), ("unit", 72), ("head", 16)]:
    CW[_n] = (_c, _c + _w)
    _c += _w
CK = _c
AW, _c = {}, 0
for _n, _w in [("w0", 128), ("router", 8), ("rbias", 8), ("b0", 1)]:
    AW[_n] = (_c, _c + _w)
    _c += _w
AK = _c
DW, _c = {}, 0
for _n, _w in [("qkv", 128), ("wout", 128), ("wp1", 128), ("wp2", 8), ("bp1", 1), ("bp2", 8), ("temp", 16),
               ("bout", 128), ("wo", 128), ("bo", 128)]:
    DW[_n] = (_c, _c + _w)
    _c += _w
DK = _c
EK = 516


class Line:

    def __init__(self, sem):
        self.sem, self.count, self.steps, self.past = sem, 0, [], {}

    def wait(self, *toks):
        for t in toks:
            if t is None:
                continue
            if isinstance(t, list):
                self.wait(*t)
                continue
            sem, v = t
            if self.past.get(sem.name, 0) < v:
                self.past[sem.name] = v
                self.steps.append(lambda e, s=sem, n=v: e.wait_ge(s, n))

    def do(self, fn, *toks):
        self.wait(*toks)
        self.steps.append(fn)

    def tell(self, fn, *toks):
        self.wait(*toks)
        self.count += 1
        self.steps.append(lambda e, f=fn: f(e).then_inc(self.sem, 1))
        return (self.sem, self.count)

    def dma(self, fn, box, *toks):
        self.wait(*toks)
        box[1] += 16
        self.steps.append(lambda e, f=fn, s=box[0]: f(e).then_inc(s, 16))
        return (box[0], box[1])

    def run(self, e):
        for s in self.steps:
            s(e)


def mm(out, lhsT, rhs, start=True, stop=True):
    return lambda e: e.matmul(out, lhsT, rhs, start=start, stop=stop)


def tr(out, in_, ident):
    return lambda e: e.transpose(out, in_, ident)


def act(out, in_, func, bias=0.0, scale=1.0, accum=None):
    if accum is None:
        return lambda e: e.activation(out, in_, func, bias=bias, scale=scale)
    return lambda e: e.activation(out, in_, func, bias=bias, scale=scale, accum_out=accum)


def cp(out, in_):
    return lambda e: e.tensor_copy(out, in_)


def tt(out, a, b, op):
    return lambda e: e.tensor_tensor(out, a, b, op)


def ts(out, a, s1, s2=None, op0=ALU.mult, op1=None):
    if op1 is None:
        return lambda e: e.tensor_scalar(out, a, s1, None, op0)
    return lambda e: e.tensor_scalar(out, a, s1, s2, op0, op1)


def stt(out, a, s, b, op0, op1):
    return lambda e: e.scalar_tensor_tensor(out=out, in0=a, scalar=s, in1=b, op0=op0, op1=op1)


def ttr(out, a, b, op0, op1, init, accum):
    return lambda e: e.tensor_tensor_reduce(out, a, b, 1.0, init, op0, op1, accum)


def red(out, a, op, negate=False):
    if negate:
        return lambda e: e.tensor_reduce(out, a, AX, op, negate=True)
    return lambda e: e.tensor_reduce(out, a, AX, op)


def rcp(out, a):
    return lambda e: e.reciprocal(out, a)


def scan(out, a, b):
    return lambda e: e.tensor_tensor_scan(out, a, b, 0.0, ALU.mult, ALU.add)


def bc(ap, shape):
    return ap.unsqueeze(len(shape) - 1).broadcast_to(shape)


def program(nc, D, out):
    with ExitStack() as ctx:
        def sb(name, shape, dt=F32):
            return ctx.enter_context(nc.sbuf_tensor(name, shape, dt))

        def sem(name):
            return ctx.enter_context(nc.semaphore(name))

        X = sb("X", [128, NT, 128])
        XA = sb("XA", [128, NT, ROW])
        XB = sb("XB", [128, NT, ROW])
        XT = sb("XT", [128, NT * 128])
        FT = sb("FT", [128, NT * 128])
        F = sb("F", [128, NT, 128])
        S = sb("S", [128, NT, 128])
        SH = sb("SH", [128, NT, 128])
        C = sb("C", [128, CK])
        WA = sb("WA", [128, AK])
        WB = sb("WB", [128, 768])
        WE = sb("WE", [128, NE * 768])
        WD = sb("WD", [128, DK])
        DI = sb("DI", [128, 64], I32)
        E = sb("E", [128, 2, 2, 256])
        PR = sb("PR", [128, 2, 2, 256])
        PT = sb("PT", [128, 2, 2, 256])
        ST = sb("ST", [128, NT, 6])
        MV = sb("MV", [128, NT, 2])
        RS = sb("RS", [128, NT])
        NM = sb("NM", [128, NT])
        SU = sb("SU", [128, NT])
        EPSB = sb("EPSB", [128, 1])
        BFC = sb("BFC", [128, 3, 256], BF16)
        RW = sb("RW", [128, 12, 32])
        POS = sb("POS", [128, 2, NT], I32)
        NI = sb("NI", [128, 2, 8], I32)
        EU = sb("EU", [128, 72])
        EUI = sb("EUI", [128, 72], I32)
        ONE = sb("ONE", [128, 256])
        ZB = sb("ZB", [128, ROW])
        XS = sb("XS", [128, 4, 4, ROW])
        XG = sb("XG", [128, 2, 512])
        HT = sb("HT", [128, 3, 256])
        YS = sb("YS", [128, 8, 128])
        SG = FT[:, 0:1536].rearrange("p (a b) -> p a b", a=3)
        HH = FT[:, 1536:3072].rearrange("p (a b) -> p a b", a=3)
        XB_flat = XB[:, :, :].rearrange("p t r -> p (t r)")
        xs_flat = XS[:, :, :, :].rearrange("p a b c -> p (a b c)")
        xg_flat = XG[:, :, :].rearrange("p a b -> p (a b)")
        R8 = xs_flat[:, 0:2048].rearrange("p (a b) -> p a b", a=8)
        WS = xs_flat[:, 0:4 * EK].rearrange("p (a b) -> p a b", a=4)
        UC = xg_flat[:, 0:504].rearrange("p (u e) -> p u e", e=7)
        JK = xg_flat.rearrange("p (a b) -> p a b", a=4)
        PXP = YS[:, :, :].rearrange("p (a b) d -> p a b d", a=2)
        WE2 = WE[:, 0:4096]
        YC = XB_flat[:, 0:8 * 512].rearrange("p (b q d) -> p b q d", b=8, q=4)
        OT = WE[:, 4096:5120].rearrange("p (a b) -> p a b", a=2)
        LG = WE[:, 5120:5632].rearrange("p (c i h) -> p c i h", c=8, i=4)
        HB = WE[:, 5632:5888].rearrange("p (b h) -> p b h", h=16)
        MX = WE[:, 5888:5952].rearrange("p (c m) -> p c m", c=8)
        SM = sb("SM", [128, 8, 32])
        A1 = sb("A1", [128, 16])
        SEL = sb("SEL", [16, 6, 8])
        SELI = sb("SELI", [16, 8], U32)
        BO3 = sb("BO3", [128, 128])
        PS = [ctx.enter_context(nc.psum_tensor(f"PS{i}", [128, 512], F32)) for i in range(8)]

        xs = nc.dram_tensor("xs_scratch", [NG * 4 * 128, ROW], F32, kind="Internal").ap()
        yc = nc.dram_tensor("yc_scratch", [NB * 128 * 4, 128], F32, kind="Internal").ap()

        def c_(n):
            return C[:, CW[n][0]:CW[n][1]]

        def a_(n):
            return WA[:, AW[n][0]:AW[n][1]]

        def d_(n):
            return WD[:, DW[n][0]:DW[n][1]]

        ident = c_("ident")
        pe, dve, sc, po, sp = (Line(sem(n)) for n in ("pe", "dve", "act", "pool", "sp"))
        box = {}

        def dsem(name):
            if name not in box:
                box[name] = [sem("d_" + name), 0]
            return box[name]

        def load(dst, src, name, *toks):
            return sp.dma(lambda e: e.dma_start(dst, src), dsem(name), *toks)

        def tile(T, t, n=1):
            return T[:, t * 128:(t + n) * 128]

        free = [None] * 8

        x_in = []

        def load_x(c):
            for b in (2 * c, 2 * c + 1):
                tok = load(X[:, 2 * b:2 * b + 2, :].rearrange("p i d -> p (i d)"),
                           D["x"][b].rearrange("(p i) d -> p (i d)", i=2), f"x{c}")
            x_in.append(tok)

        load_x(0)
        l_id = load(C[:, 0:128], D["consts"][:, 0:128], "id")
        l_wa = load(WA[:, :], D["wa"], "wa")
        load_x(1)
        for c in range(2, 8):
            load_x(c)
        l_c = load(C[:, 128:CK], D["consts"][:, 128:CK], "c")
        l_di = load(DI[:, :], D["dest"], "di")
        z1 = po.tell(lambda e: e.memset(ZB[:, :], 0.0))
        z2 = po.tell(lambda e: e.memset(ZB[:, 128:129].bitcast(I32), NOWHERE), z1)
        l_fill = load(xs.rearrange("(u p) r -> p u r", p=128), ZB[:, :].unsqueeze(1).broadcast_to([128, NG * 4, ROW]),
                      "fill", z2, x_in)
        l_wb = load(WB[:, :], D["wb"], "wb")
        l_we = load(WE[:, :], D["we"], "we")
        l_wd = load(WD[:, :], D["wd"], "wd")

        k_eps = po.tell(lambda e: e.memset(EPSB[:, :], EPS))
        k_one = po.tell(lambda e: e.memset(ONE[:, :], 1.0))
        k_bf1 = po.tell(lambda e: e.memset(BFC[:, 1, :], 1.0))

        def stats(T, t0, n, *toks):
            def one(t):
                return lambda e: e.bn_stats(ST[:, t, :], T[:, t, :])

            def two_(t):
                return lambda e: e.bn_aggr(MV[:, t, :], ST[:, t, :])
            a = [dve.tell(one(t), *toks) for t in range(t0, t0 + n)]
            return [dve.tell(two_(t), a[t - t0]) for t in range(t0, t0 + n)][-1]

        xt_done, xa_done, xb_done, sd_done = [], [], [], []

        def spread_in(c):
            t0 = 4 * c
            mv = stats(X, t0, 4, x_in[c])
            sd_done.append(sc.tell(act(RS[:, t0:t0 + 4], MV[:, t0:t0 + 4, 1], ACT.Sqrt, bias=EPSB[:, :]), mv, k_eps))

        def norm_in(c):
            t0 = 4 * c
            rs = dve.tell(rcp(RS[:, t0:t0 + 4], RS[:, t0:t0 + 4]), sd_done[c])
            for t in range(t0, t0 + 4):
                xa = dve.tell(ts(XA[:, t, 0:128], X[:, t, :], MV[:, t, 0:1], RS[:, t:t + 1], ALU.subtract, ALU.mult), rs)
            xa_done.append(xa)

        def turn_in(c):
            k = c % 2
            for j in range(4):
                tok = pe.tell(tr(PS[k][:, j * 128:(j + 1) * 128], XA[:, 4 * c + j, 0:128], ident), xa_done[c], l_id, free[k])
            free[k] = sc.tell(act(tile(XT, 4 * c, 4), PS[k][:, :], ACT.Copy), tok)
            xt_done.append(free[k])

        ft_done, f_done = [], []

        def logits(c):
            for t in range(4 * c, 4 * c + 4):
                tok = pe.tell(mm(PS[2][:, 8 * t:8 * t + 8], tile(XT, t), a_("router")), xt_done[c], l_wa)
            return tok

        def project(c):
            k = 3 + c % 2
            ft = pe.tell(mm(PS[k][:, :], a_("w0"), tile(XT, 4 * c, 4)), free[k])
            free[k] = sc.tell(act(tile(FT, 4 * c, 4), PS[k][:, :], ACT.Identity, bias=a_("b0")), ft, l_wa)
            ft_done.append(free[k])

        def turn_f(c):
            k = 5 + c % 2
            for j in range(4):
                tok = pe.tell(tr(PS[k][:, j * 128:(j + 1) * 128], tile(FT, 4 * c + j), ident), ft_done[c], free[k])
            free[k] = sc.tell(act(F[:, 4 * c:4 * c + 4, :], PS[k][:, :].rearrange("p (t d) -> p t d", d=128), ACT.Copy), tok)
            f_done.append(free[k])

        EARLY = 4
        spread_in(0)
        for i in range(8 + 2):
            if i + 1 < 8:
                spread_in(i + 1)
            if i < 8:
                norm_in(i)
            if 1 <= i < 9:
                turn_in(i - 1)
            if 2 <= i:
                lg = logits(i - 2)
                if i - 2 < EARLY:
                    project(i - 2)
            if 3 <= i < EARLY + 3:
                turn_f(i - 3)
        for c in range(8):
            xb_done.append(po.tell(cp(XB[:, 4 * c:4 * c + 4, 0:128], XA[:, 4 * c:4 * c + 4, 0:128]), xa_done[c]))

        def et(ap):
            return ap.rearrange("p (e t) -> p e t", e=NE)

        def te(ap):
            return ap.rearrange("p (e t) -> p t e", e=NE)

        def over_e(ap):
            return ap.unsqueeze(1).broadcast_to([128, NE, NT])

        lgs, prob, eq, cand, oh1, oh2, ex, pos = (R8[:, i, :] for i in range(8))
        m1, m2, i1, i2, rw, w1, w2 = (RW[:, i, :] for i in range(7))
        base = RW[:, 8:12, :].rearrange("p a b -> p (a b)")
        n_e, pad, cum, corr = (base[:, 8 * i:8 * i + 8] for i in range(4))

        upper = dve.tell(cp(BFC[:, 0, 0:128], c_("upper")), l_c)
        q = dve.tell(tt(et(lgs), PS[2][:, 0:256].rearrange("p (t e) -> p e t", e=NE), bc(a_("rbias"), [128, NE, NT]),
                        ALU.add), lg, l_wa)
        free[2] = q
        q = sc.tell(act(prob, lgs, ACT.Sigmoid), q)
        for c in range(EARLY, 8):
            project(c)
            if c > EARLY:
                turn_f(c - 1)
        turn_f(7)
        dve.do(cp(XA[:, :, 128].bitcast(I32), DI[:, 0:32]), l_di, xa_done)
        cols = dve.tell(cp(XB[:, :, 128].bitcast(I32), DI[:, 32:64]))

        def top(p, m, i, oh, tok):
            tok = dve.tell(red(m, te(p), ALU.max), tok)
            tok = dve.tell(tt(et(eq), et(p), over_e(m), ALU.is_equal), tok)
            tok = dve.tell(tt(cand, eq, c_("e8"), ALU.mult), tok)
            tok = dve.tell(red(i, te(cand), ALU.min), tok)
            return dve.tell(tt(et(oh), et(c_("e8")), over_e(i), ALU.is_equal), tok)

        q = top(prob, m1, i1, oh1, q)
        q = dve.tell(stt(lgs, oh1, -2.0, prob, ALU.mult, ALU.add), q)
        q = top(lgs, m2, i2, oh2, q)
        mask = dve.tell(tt(BFC[:, 2, :], oh1, oh2, ALU.add), q)
        r1 = pe.tell(mm(PS[7][:, 0:256], BFC[:, 0, 0:128], BFC[:, 2, :]), mask, upper, free[7])
        r2 = pe.tell(mm(PS[7][:, 256:512], BFC[:, 1, 0:128], BFC[:, 2, :]), k_bf1)
        within, total = PS[7][:, 0:256], PS[7][:, 256:512]
        w = dve.tell(tt(rw, m1, m2, ALU.add))
        w = dve.tell(rcp(rw, rw), w)
        dve.do(tt(XA[:, :, 129], m1, rw, ALU.mult), w, *xa_done)
        cols = dve.tell(tt(XB[:, :, 129], m2, rw, ALU.mult))
        q = dve.tell(scan(cand, ONE[:, :], total), r2, k_one)
        q = dve.tell(tt(ex, cand, total, ALU.subtract), q)
        q = dve.tell(tt(n_e, et(cand)[:, :, 31], et(ex)[:, :, 0], ALU.subtract), q)
        q = dve.tell(ts(NI[:, 0, :], n_e, 127.0, None, ALU.add), q)
        q = dve.tell(ts(NI[:, 1, :], NI[:, 0, :], -128, None, ALU.bitwise_and), q)
        q = dve.tell(cp(pad, NI[:, 1, :]), q)
        cq = dve.tell(scan(cum, ONE[:, 0:8], pad), q)
        q = dve.tell(tt(corr, cum, pad, ALU.subtract), cq)
        q = dve.tell(tt(corr, corr, et(ex)[:, :, 0], ALU.subtract), q)
        free[7] = dve.tell(tt(pos, within, ex, ALU.add), q)
        q = dve.tell(tt(et(pos), et(pos), bc(corr, [128, NE, NT]), ALU.add), free[7])
        q1 = dve.tell(tt(oh1, oh1, pos, ALU.mult), q)
        q2 = dve.tell(tt(oh2, oh2, pos, ALU.mult), q)
        dve.do(red(w1, te(oh1), ALU.add), q1)
        q = dve.tell(red(w2, te(oh2), ALU.add), q2)
        places = dve.tell(cp(POS[:, :, :], RW[:, 5:7, :]), q)
        q = dve.tell(tt(UC[:, :, :], bc(c_("unit"), [128, 72, 7]), cum[:, 0:7].unsqueeze(1).broadcast_to([128, 72, 7]),
                        ALU.is_ge), cq)
        q = dve.tell(red(EU[:, :], UC[:, :, :], ALU.add), q)
        experts = dve.tell(ts(EUI[:, :], EU[:, :], 768.0, None, ALU.mult), q)

        def scatter(dst, idx, src, name, bound, *toks):
            return po.dma(lambda e: e.indirect_dma_start(
                out=dst, out_offset=bass.IndirectOffsetOnAxis(ap=idx, axis=0), in_=src, in_offset=None,
                bounds_check=bound, oob_is_err=False), dsem(name), *toks)

        po.wait(places, cols, l_fill, *xb_done)
        for t in range(NT):
            scatter(xs, POS[:, 0, t:t + 1], XA[:, t, :], "disp", NG * 4 * 128 - 1)
            dispatched = scatter(xs, POS[:, 1, t:t + 1], XB[:, t, :], "disp", NG * 4 * 128 - 1)

        sc_done, ex_done, pt_done = {}, {}, {}
        pv_read, s_done = {}, {}

        def scores(b):
            k = b % 2
            for i in range(2):
                tok = pe.tell(mm(PS[k][:, i * 256:(i + 1) * 256], tile(FT, 2 * b + i), tile(FT, 2 * b, 2)),
                              ft_done[b // 2], free[k])
            for i in range(2):
                t = 2 * b + i
                e1 = dve.tell(ttr(E[:, k, i, :], PS[k][:, i * 256:(i + 1) * 256],
                                  c_("dist")[:, i * 256:(i + 1) * 256], ALU.add, ALU.max, -3.0e38, RW[:, 7, t:t + 1]),
                              tok, l_c, ex_done.get(b - 2))
            free[k] = e1
            nm = dve.tell(ts(NM[:, 2 * b:2 * b + 2], RW[:, 7, 2 * b:2 * b + 2], -1.0), e1)
            for i in range(2):
                t = 2 * b + i
                tok = sc.tell(act(PR[:, k, i, :], E[:, k, i, :], ACT.Exp, bias=NM[:, t:t + 1], accum=SU[:, t:t + 1]),
                              nm, pt_done.get(b - 2))
            ex_done[b] = tok
            sc_done[b] = dve.tell(rcp(SU[:, 2 * b:2 * b + 2], SU[:, 2 * b:2 * b + 2]), tok)

        def turn_p(b):
            k, kb = 3 + b % 2, b % 2
            for j in range(2):
                for i in range(2):
                    tok = pe.tell(tr(PS[k][:, j * 256 + i * 128:j * 256 + (i + 1) * 128],
                                     PR[:, kb, i, j * 128:(j + 1) * 128], ident), ex_done[b], free[k])
            pt_done[b] = tok
            free[k] = dve.tell(cp(PT[:, kb, :, :], PS[k][:, :].rearrange("p (j i) -> p j i", j=2)), tok, pv_read.get(b - 2))

        def mix(b):
            k, kb = 5 + b % 2, b % 2
            for i in range(2):
                for j in range(2):
                    tok = pe.tell(mm(PS[k][:, i * 128:(i + 1) * 128], PT[:, kb, j, i * 128:(i + 1) * 128],
                                     F[:, 2 * b + j, :], start=j == 0, stop=j == 1),
                                  free[3 + b % 2], free[k], f_done[b // 2])
            pv_read[b] = tok
            for i in range(2):
                t = 2 * b + i
                free[k] = sc.tell(act(S[:, t, :], PS[k][:, i * 128:(i + 1) * 128], ACT.Copy, scale=SU[:, t:t + 1]),
                                  tok, sc_done[b])
            s_done[b] = free[k]

        for i in range(NB + 2):
            if i < NB:
                scores(i)
            if 1 <= i < NB + 1:
                turn_p(i - 1)
            if i >= 2:
                mix(i - 2)

        h_done, h_read, sg_read, ehr = {}, {}, {}, {}

        def up(j):
            c, f = divmod(j, 2)
            k = 2 * (j % 2)
            g = pe.tell(mm(PS[k][:, :], WB[:, f * 128:(f + 1) * 128], tile(XT, 4 * c, 4)), l_wb, free[k])
            u = pe.tell(mm(PS[k + 1][:, :], WB[:, 256 + f * 128:256 + (f + 1) * 128], tile(XT, 4 * c, 4)), free[k + 1])
            free[k] = sc.tell(act(SG[:, j % 3, :], PS[k][:, :], ACT.Silu), g, sg_read.get(j - 3), sc_done[NB - 1],
                              sg_read.get(("e", NU - 1)))
            free[k + 1] = dve.tell(tt(HH[:, j % 3, :], SG[:, j % 3, :], PS[k + 1][:, :], ALU.mult), u, free[k],
                                   h_read.get(j - 3), ehr.get(NU - 1))
            sg_read[j] = h_done[j] = free[k + 1]

        def down(c):
            k = 4 + c % 2
            for t in range(4):
                for f in range(2):
                    tok = pe.tell(mm(PS[k][:, t * 128:(t + 1) * 128], HH[:, (2 * c + f) % 3, t * 128:(t + 1) * 128],
                                     WB[:, 512 + f * 128:512 + (f + 1) * 128], start=f == 0, stop=f == 1),
                                  h_done[2 * c + 1], free[k])
            h_read[2 * c] = h_read[2 * c + 1] = tok
            free[k] = sc.tell(act(SH[:, 4 * c:4 * c + 4, :], PS[k][:, :].rearrange("p (t d) -> p t d", d=128), ACT.Copy), tok)
            return free[k]

        def shared(c0, c1):
            for j in range(2 * c0, 2 * c1):
                up(j)
                if j % 2 == 0 and j > 2 * c0:
                    down(j // 2 - 1)
            return down(c1 - 1)

        LATE = 5
        shared(0, LATE)
        JL = 2 * LATE - 1

        xs_in, xs_read, xg_done, xg_read = {}, {}, {}, {}
        eh_done, ht_done, ht_read, y_out = {}, {}, {}, {}
        ys_done = {}
        nu = [min(4, NU - 4 * g) for g in range(NG)]

        def fetch(g):
            n = nu[g]
            xs_in[g] = load(XS[:, g % 4, 0:n, :], xs[g * 512:g * 512 + n * 128, :].rearrange("(u p) r -> p u r", p=128),
                            f"xs{g % 4}", dispatched, xs_read.get(g - 4), y_out.get(4 * (g - 4) + 3))

        def turn_x(g):
            for j in range(nu[g]):
                tok = pe.tell(tr(PS[6][:, j * 128:(j + 1) * 128], XS[:, g % 4, j, 0:128], ident), xs_in[g], free[6])
            xs_read[g] = tok
            free[6] = sc.tell(act(XG[:, g % 2, 0:nu[g] * 128], PS[6][:, 0:nu[g] * 128], ACT.Copy), tok, xg_read.get(g - 2))
            xg_done[g] = free[6]

        reg = {}

        def pick(u):
            def f(e):
                reg[u] = e.value_load(EUI[0:1, u:u + 1], min_val=0, max_val=7 * 768)
            pe.do(f, experts, l_we)

        def gate_up(u):
            g, j = divmod(u, 4)
            k = u % 3
            pick(u)
            tok = pe.tell(lambda e: e.matmul(PS[k][:, :], XG[:, g % 2, j * 128:(j + 1) * 128], WE[:, bass.ds(reg[u], 512)],
                                             start=True, stop=True), xg_done[g], free[k])
            if j == nu[g] - 1:
                xg_read[g] = tok
            a = sc.tell(act(SG[:, u % 3, 0:256], PS[k][:, 0:256], ACT.Silu), tok, sg_read.get(("e", u - 3)), sg_read[JL])
            free[k] = dve.tell(tt(HH[:, u % 3, 0:256], SG[:, u % 3, 0:256], PS[k][:, 256:512], ALU.mult), a,
                               ehr.get(u - 3), h_read[JL])
            sg_read[("e", u)] = eh_done[u] = free[k]

        def turn_h(u):
            k = 3 + u % 2
            for f in range(2):
                tok = pe.tell(tr(PS[k][:, f * 128:(f + 1) * 128], HH[:, u % 3, f * 128:(f + 1) * 128], ident),
                              eh_done[u], free[k])
            ehr[u] = tok
            free[k] = dve.tell(cp(HT[:, u % 3, :], PS[k][:, 0:256]), tok, ht_read.get(u - 3))
            ht_done[u] = free[k]

        def down_e(u):
            g, j = divmod(u, 4)
            k = (5, 7)[u % 2]
            for f in range(2):
                tok = pe.tell(lambda e, f=f: e.matmul(PS[k][:, 0:128], HT[:, u % 3, f * 128:(f + 1) * 128],
                                                      WE[:, bass.ds(reg[u] + (512 + f * 128), 128)],
                                                      start=f == 0, stop=f == 1), ht_done[u], free[k])
            ht_read[u] = tok
            free[k] = sc.tell(act(YS[:, u % 8, :], PS[k][:, 0:128], ACT.Copy, scale=XS[:, g % 4, j, 129:130]), tok,
                              y_out.get(u - 8))
            ys_done[u] = free[k]
            y_out[u] = scatter(yc, XS[:, g % 4, j, 128:129].bitcast(U32), YS[:, u % 8, :], f"y{u % 8}", NB * 128 * 4 - 1,
                               ys_done[u])

        for g in range(3):
            fetch(g)
        turn_x(0)
        for u in range(NU + 3):
            if u < NU:
                gate_up(u)
                if u % 4 == 2 and u // 4 + 1 < NG:
                    turn_x(u // 4 + 1)
                if u % 4 == 3 and u // 4 + 3 < NG:
                    fetch(u // 4 + 3)
            if 2 <= u < NU + 2:
                turn_h(u - 2)
            if u >= 3:
                down_e(u - 3)
        routed = [y_out[u] for u in range(NU - 8, NU)]
        sh_done = shared(LATE, 8)

        NC = 8
        WT, W2, XNB = FT, WE2, SH
        yin, yt_read = {}, {}
        x1_mid, xn_done, xt1_done = {}, {}, {}
        bo3 = dve.tell(ts(BO3[:, :], d_("bo"), 0.3), l_wd)
        half_b = dve.tell(ts(d_("bout"), d_("bout"), 0.5), l_wd)

        def four(T, c):
            return T[:, 4 * c:4 * c + 4, 0:128]

        def collect(c):
            for b in (2 * c, 2 * c + 1):
                yin[c] = load(YC[:, b % 8, :, :].rearrange("p q d -> p (q d)"),
                              yc.rearrange("(b p q) d -> b p (q d)", b=NB, q=4)[b], f"yt{b % 8 // 2}",
                              routed, yt_read.get(c - 4), dispatched)

        def end0(c):
            y = YC[:, 2 * (c % 4):2 * (c % 4) + 2, :, :].rearrange("p b (i s) d -> p b i s d", s=2)
            F4 = four(F, c).rearrange("p (b i) d -> p b i d", b=2)
            e = po if c % 2 else dve
            a = e.tell(tt(F4, y[:, :, :, 0, :], y[:, :, :, 1, :], ALU.add), yin[c], pv_read[NB - 1])
            yt_read[c] = a
            return a

        def gate0(c, a):
            t = dve.tell(tt(four(SH, c), four(SH, c), four(F, c), ALU.add), a, sh_done)
            return sc.tell(act(four(F, c), four(SH, c), ACT.Silu), t)

        def rest0(c):
            m = po.tell(tt(four(F, c), four(F, c), four(S, c), ALU.mult), gated[c], s_done[NB - 1])
            x1 = po.tell(tt(four(X, c), four(X, c), four(F, c), ALU.add), m)
            mv = stats(X, 4 * c, 4, x1)
            t = slice(4 * c, 4 * c + 4)
            rooted[c] = sc.tell(act(RS[:, t], MV[:, t, 1], ACT.Sqrt, bias=EPSB[:, :]), mv)

        def norm1(c):
            r = slice(4 * c, 4 * c + 4)
            rs = dve.tell(rcp(RS[:, r], RS[:, r]), rooted[c])
            for t in range(4 * c, 4 * c + 4):
                xn_done[c] = dve.tell(ts(XA[:, t, 0:128], X[:, t, :], MV[:, t, 0:1], RS[:, t:t + 1], ALU.subtract,
                                         ALU.mult), rs)

        def turn1(c):
            k = c % 2
            for i in range(4):
                tok = pe.tell(tr(PS[k][:, i * 128:(i + 1) * 128], XA[:, 4 * c + i, 0:128], ident), xn_done[c], free[k])
            free[k] = sc.tell(act(tile(XT, 4 * c, 4), PS[k][:, :], ACT.Copy), tok)
            xt1_done[c] = free[k]

        N2, RN, DOT, SPI = (SM[:, i, 0:16] for i in range(4))
        HM = SM[:, 4, 0:16]
        hm = dve.tell(tt(HM, c_("head"), d_("temp"), ALU.mult), l_wd, l_c)
        w_done, hb_done, lg_done, px_done, px_read, ot_done, ot_read, s1_done, w2_read = ({} for _ in range(9))
        heads_in, heads_out, n2_done, heads_ps = {}, {}, {}, {}

        def w2v(b):
            return W2[:, b * 256:(b + 1) * 256]

        def proj(c):
            k = 2 + c % 2
            tok = pe.tell(mm(PS[k][:, :], d_("qkv"), tile(XT, 4 * c, 4)), xt1_done[c], l_wd, free[k])
            for h in range(2):
                b = 2 * c + h
                n2 = sc.tell(act(w2v(b), PS[k][:, h * 256:(h + 1) * 256], ACT.Square, accum=N2[:, b:b + 1]),
                             tok, routed)
            free[k] = sc.tell(act(tile(WT, 4 * c, 4), PS[k][:, :], ACT.Copy), routed, h_read[15])
            w_done[c] = free[k]
            n2_done[c] = n2

        def weigh(c):
            bb, n2 = slice(2 * c, 2 * c + 2), n2_done[c]
            r = dve.tell(ts(RN[:, bb], N2[:, bb], 1e-24, None, ALU.max), n2)
            r = dve.tell(rcp(RN[:, bb], RN[:, bb]), r)
            hb_done[c] = dve.tell(tt(HB[:, bb, :], HM.unsqueeze(1).broadcast_to([128, 2, 16]),
                                     bc(RN[:, bb], [128, 2, 16]), ALU.mult), r, hm)

        def heads(c):
            k = 4 + c % 2
            for i in range(4):
                b = 2 * c + i // 2
                tok = pe.tell(mm(PS[k][:, i * 16:(i + 1) * 16], w2v(b)[:, i % 2 * 128:(i % 2 + 1) * 128], HB[:, b, :]),
                              hb_done[c], free[k])
            heads_ps[c] = tok

        def center(c):
            k = 4 + c % 2
            lg = PS[k][:, 0:64].rearrange("p (i h) -> p i h", i=4)
            m = dve.tell(red(MX[:, c, 0:4], lg, ALU.max), heads_ps[c])
            free[k] = dve.tell(tt(LG[:, c, :, :], lg, bc(MX[:, c, 0:4], [128, 4, 16]), ALU.subtract), m)
            heads_in[c] = free[k]

        def soft(c):
            heads_out[c] = sc.tell(act(LG[:, c, :, :], LG[:, c, :, :], ACT.Exp), heads_in[c])

        def share(c):
            m = dve.tell(red(MX[:, c, 4:8], LG[:, c, :, :], ALU.add), heads_out[c])
            m = dve.tell(rcp(MX[:, c, 4:8], MX[:, c, 4:8]), m)
            px_done[c] = dve.tell(tt(PXP[:, c % 2, :, :].rearrange("p i (h d) -> p i h d", d=8),
                                     bc(LG[:, c, :, :], [128, 4, 16, 8]),
                                     MX[:, c, 4:8].unsqueeze(2).unsqueeze(3).broadcast_to([128, 4, 16, 8]), ALU.mult),
                                  m, px_read.get(c - 2))

        def spread(c):
            k, ks = c % 2, 6
            for i in range(4):
                tok = pe.tell(tr(PS[k][:, i * 128:(i + 1) * 128], PXP[:, c % 2, i, :], ident), px_done[c], free[k])
            for i in range(4):
                t2 = pe.tell(mm(PS[ks][:, i // 2:i // 2 + 1], PXP[:, c % 2, i, :], ONE[:, 0:1], start=i % 2 == 0,
                                stop=i % 2 == 1), free[ks])
            px_read[c] = t2
            bb = slice(2 * c, 2 * c + 2)
            q = dve.tell(ts(SPI[:, bb], PS[ks][:, 0:2], 1e-8, None, ALU.add), t2)
            free[ks] = q
            d = []
            for h in range(2):
                b = 2 * c + h
                d.append(dve.tell(ttr(JK[:, b % 4, :], PS[k][:, h * 256:(h + 1) * 256], w2v(b), ALU.mult, ALU.add, 0.0,
                                      DOT[:, b:b + 1]), tok))
            q = dve.tell(rcp(SPI[:, bb], SPI[:, bb]), q)
            q = dve.tell(tt(DOT[:, bb], DOT[:, bb], SPI[:, bb], ALU.mult), q, d)
            q = dve.tell(ts(DOT[:, bb], DOT[:, bb], 1.0, None, ALU.add), q)
            q = dve.tell(rcp(DOT[:, bb], DOT[:, bb]), q)
            for h in range(2):
                b = 2 * c + h
                free[k] = dve.tell(stt(OT[:, c % 2, h * 256:(h + 1) * 256], PS[k][:, h * 256:(h + 1) * 256],
                                       DOT[:, b:b + 1], tile(WT, 2 * b, 2), ALU.mult, ALU.mult),
                                   q, w_done[c], ot_read.get(c - 2))
            ot_done[c] = free[k]

        def out1(c):
            k = 7
            for i in range(4):
                tok = pe.tell(mm(PS[k][:, i * 128:(i + 1) * 128], OT[:, c % 2, i * 128:(i + 1) * 128], d_("wout")),
                              ot_done[c], free[k])
            ot_read[c] = tok
            free[k] = dve.tell(stt(four(S, c), PS[k][:, :].rearrange("p (i d) -> p i d", d=128), -0.5,
                                   d_("bout").unsqueeze(1).broadcast_to([128, 4, 128]), ALU.mult, ALU.add), tok, half_b)
            s1_done[c] = free[k]

        for c in range(4):
            collect(c)
        gated, rooted, halves_in = {}, {}, {}
        for c in range(NC + 1):
            if c < NC:
                halves_in[c] = end0(c)
                if c + 4 < NC:
                    collect(c + 4)
            if c:
                gated[c - 1] = gate0(c - 1, halves_in[c - 1])
        for i in range(NC + 1):
            if i < NC:
                rest0(i)
            if 1 <= i:
                norm1(i - 1)
            if 3 <= i:
                weigh(i - 3)
            if 4 <= i:
                center(i - 4)
            if 1 <= i:
                turn1(i - 1)
            if 2 <= i:
                proj(i - 2)
            if 3 <= i:
                heads(i - 3)
        tok = pe.tell(mm(PS[7][:, 0:16], d_("wp1"), XT[:, 255::256]), l_wd, [xt1_done[c] for c in range(NC)], free[7])
        a1 = sc.tell(act(A1[:, :], PS[7][:, 0:16], ACT.Gelu, bias=d_("bp1")), tok)
        proj(7)
        weigh(6)
        heads(6)
        center(5)
        tok = pe.tell(mm(PS[7][0:16, 0:8], A1[:, :], d_("wp2")), a1)
        lt = SEL[:, 0, :]
        tok = dve.tell(tt(lt, PS[7][0:16, 0:8], d_("bp2")[0:16, :], ALU.add), tok)
        free[7] = tok
        tok = dve.tell(red(SEL[:, 1, 0:1], lt, ALU.max, negate=True), tok)
        tok = sc.tell(act(SEL[:, 2, :], lt, ACT.Exp, bias=SEL[:, 1, 0:1], accum=SEL[:, 3, 0:1]), tok)
        early = 6
        for c in range(early):
            soft(c)
        weigh(7)
        center(6)
        heads(7)
        tok = dve.tell(rcp(SEL[:, 3, 0:1], SEL[:, 3, 0:1]), tok)
        tok = dve.tell(ts(SEL[:, 2, :], SEL[:, 2, :], SEL[:, 3, 0:1]), tok)
        tok = dve.tell(lambda e: e.max(SEL[:, 4, :], SEL[:, 2, :]), tok)
        chosen = dve.tell(lambda e: e.max_index(SELI[:, :], SEL[:, 4, :], SEL[:, 2, :]), tok)
        ws_in, ws_read = {}, {}

        def expert1(b):
            s = b % 4

            def f(e):
                v = e.value_load(SELI[b:b + 1, 0:1], min_val=0, max_val=7)
                return e.dma_start(WS[:, s, :], D["w1"][bass.ds(v, 1)].rearrange("o p k -> p (o k)"))
            ws_in[b] = sp.dma(f, dsem(f"ws{s}"), chosen, routed, ws_read.get(b - 4))

        for b in range(4):
            expert1(b)

        H1 = E
        RT = PT
        xnb_done, h1_done, h1_read, rt_done, rt_read, t_done = {}, {}, {}, {}, {}, {}
        for c in range(NC):
            xnb_done[c] = po.tell(tt(four(XNB, c), four(XA, c), BO3[:, :].unsqueeze(1).broadcast_to([128, 4, 128]), ALU.add),
                                  xn_done[c], bo3)

        def ff_up(b):
            k, s = 2 + b % 2, b % 4
            for f in range(2):
                tok = pe.tell(mm(PS[k][:, f * 256:(f + 1) * 256], WS[:, s, f * 128:(f + 1) * 128], tile(XT, 2 * b, 2)),
                              ws_in[b], free[k])
            for f in range(2):
                free[k] = sc.tell(act(H1[:, b % 2, f, :], PS[k][:, f * 256:(f + 1) * 256], ACT.Gelu,
                                      bias=WS[:, s, 512 + f:513 + f]), tok, h1_read.get(b - 2))
            h1_done[b] = free[k]

        def ff_down(b):
            k, s = 4, b % 4
            for f in range(2):
                tok = pe.tell(mm(PS[k][:, 0:256], WS[:, s, 256 + f * 128:256 + (f + 1) * 128], H1[:, b % 2, f, :],
                                 start=f == 0, stop=f == 1), h1_done[b], free[k])
            h1_read[b] = tok
            free[k] = sc.tell(act(RT[:, b % 2, 0, :], PS[k][:, 0:256], ACT.Identity, bias=WS[:, s, 514:515]), tok,
                              rt_read.get(b - 2))
            rt_done[b] = ws_read[b] = free[k]
            if b + 4 < NB:
                expert1(b + 4)

        def ff_out(b):
            k, h, c = 6 if b == NB - 1 else 5, b % 2, b // 2
            for i in range(2):
                tok = pe.tell(mm(PS[k][:, (2 * h + i) * 128:(2 * h + i + 1) * 128], RT[:, b % 2, 0, i * 128:(i + 1) * 128],
                                 d_("wo")), rt_done[b], free[k])
            rt_read[b] = tok
            v = [PS[k][:, 256 * i:256 * i + 256].rearrange("p (i d) -> p i d", i=2) for i in range(2)]
            if c == NC - 1:
                t_done[b] = dve.tell(stt(XNB[:, 2 * b:2 * b + 2, :], v[h], 0.3, XNB[:, 2 * b:2 * b + 2, :], ALU.mult, ALU.add),
                                     tok, xnb_done[c])
                free[k] = t_done[b]
            elif h == 1:
                free[k] = dve.tell(stt(four(XNB, c), PS[k][:, :].rearrange("p (i d) -> p i d", i=4), 0.3,
                                       four(XNB, c), ALU.mult, ALU.add), tok, xnb_done[c])
                t_done[b - 1] = t_done[b] = free[k]

        stored, finished = [], []

        def end1(b, n, last):
            r = slice(2 * b, 2 * b + 2 * n)
            g = sc.tell(act(F[:, r, :], XNB[:, r, :], ACT.Tanh, scale=0.5), t_done[b])
            g = dve.tell(stt(F[:, r, :], F[:, r, :], 1.0, XNB[:, r, :], ALU.add, ALU.mult), g)
            e = dve if last else po
            m = e.tell(tt(F[:, r, :], F[:, r, :], S[:, r, :], ALU.mult), g, s1_done[b // 2])
            a = e.tell(tt(X[:, r, :], X[:, r, :], F[:, r, :], ALU.add), m)
            for i in range(b, b + n):
                finished.append((i, a))

        def store():
            while finished:
                i, a = finished.pop(0)
                stored.append(load(out[i].rearrange("(p i) d -> p (i d)", i=2),
                                   X[:, 2 * i:2 * i + 2, :].rearrange("p i d -> p (i d)"), "out", a))

        share(0)
        share(1)
        center(7)
        for c in range(early, NC):
            soft(c)
        for b in range(NB + 3):
            if b % 2 == 0 and b < NB:
                c = b // 2
                spread(c)
                if c + 2 < NC:
                    share(c + 2)
            if b < NB:
                ff_up(b)
            if b % 2 == 1 and b < NB:
                out1(b // 2)
            if 1 <= b < NB + 1:
                ff_down(b - 1)
            if 2 <= b < NB + 2:
                ff_out(b - 2)
            if b >= 4 and b % 2 == 0 and b < NB + 2:
                store()
                end1(b - 4, 2, False)
            if b >= NB + 1:
                end1(b - 3, 1, True)
                store()
        sp.wait(stored[-1], dispatched, l_fill, [y_out[u] for u in range(NU)])

        block = ctx.enter_context(nc.Block())

        @block.sync
        def _(e):
            sp.run(e)

        @block.tensor
        def _(e):
            pe.run(e)

        @block.vector
        def _(e):
            dve.run(e)

        @block.scalar
        def _(e):
            sc.run(e)

        @block.gpsimd
        def _(e):
            po.run(e)


def constants():
    p = np.arange(128)
    c = np.zeros((128, CK), np.float32)

    def put(name, a):
        c[:, CW[name][0]:CW[name][1]] = a
    put("ident", np.eye(128, dtype=np.float32))
    i = 2 * p[:, None, None, None] + np.arange(2)[None, :, None, None]
    j = 2 * p[None, None, None, :] + np.arange(2)[None, None, :, None]
    put("dist", (np.clip(np.abs(i - j), 0, 10).astype(np.float32) * np.float32(0.01)).reshape(128, 512))
    put("upper", (p[:, None] < p[None, :]).astype(np.float32))
    put("e8", np.repeat(np.arange(8) - 8, 32).astype(np.float32)[None, :])
    put("unit", (128 * np.arange(72)).astype(np.float32)[None, :])
    put("head", (p[:, None] // 8 == np.arange(16)[None, :]).astype(np.float32))
    t = np.arange(NT)
    slot0 = ((t[None, :] // 2 * 128 + p[:, None]) * 4 + 2 * (t[None, :] % 2)).astype(np.int32)
    return c, np.concatenate([slot0, slot0 + 1], axis=1).astype(np.int32)


def layout(a):
    def rep(v):
        return np.broadcast_to(v.reshape(1, -1), (128, v.size))

    def halves(m):
        return np.concatenate([m[0:128], m[128:256]], axis=1)

    consts, dest = constants()
    wa = np.concatenate([a["L0_attn_W"].T, a["L0_ffn_router_w"].T, rep(a["L0_ffn_routing_bias"]),
                         a["L0_attn_b"].reshape(128, 1)], axis=1)
    wb = np.concatenate([a["L0_ffn_shared_gate"].T, a["L0_ffn_shared_up"].T, halves(a["L0_ffn_shared_down"].T)], axis=1)
    we = np.concatenate([np.concatenate([a["L0_ffn_gate_w"][e], a["L0_ffn_up_w"][e], halves(a["L0_ffn_down_w"][e])], axis=1)
                         for e in range(8)], axis=1)
    temp = a["L1_attn_temp"].reshape(16)
    wd = np.concatenate([a["L1_attn_Wqkv"].T, a["L1_attn_Wout"].T, a["L1_ffn_Wp1"], a["L1_ffn_Wp2"],
                         a["L1_ffn_bp1"].reshape(128, 1), rep(a["L1_ffn_bp2"]), rep(temp), rep(a["L1_attn_bout"]),
                         a["L1_ffn_Wo"], rep(a["L1_ffn_bo"])], axis=1)
    w1 = np.stack([np.concatenate([a["L1_ffn_W1"][e], halves(a["L1_ffn_W2"][e]), a["L1_ffn_b1"][e].reshape(2, 128).T,
                                   a["L1_ffn_b2"][e].reshape(128, 1), np.zeros((128, 1), np.float32)], axis=1)
                   for e in range(8)])
    return {"x": a["L0_attn_x"], "consts": consts, "dest": dest, "wa": wa, "wb": wb, "we": we, "wd": wd, "w1": w1}


def kernel(**inputs):
    import concourse.bacc as bacc
    from concourse.bass_utils import run_bass_kernel_spmd as run

    nc = bacc.Bacc("TRN2", target_bir_lowering=False, num_devices=1)
    arrays = {n: np.ascontiguousarray(v) for n, v in layout({k: np.asarray(v) for k, v in inputs.items()}).items()}
    aps = {n: nc.dram_tensor(f"in_{n}", v.shape, mybir.dt.from_np(v.dtype), kind="ExternalInput").ap()
           for n, v in arrays.items()}
    out = nc.dram_tensor("out_0", (16, 256, 128), F32, kind="ExternalOutput").ap()
    program(nc, aps, out)
    r = run(nc, [{f"in_{n}": v for n, v in arrays.items()}], core_ids=[0])
    return r.results[0]["out_0"]
```

```python
from contextlib import ExitStack

import numpy as np

import concourse.bass as bass
from concourse import mybir

F32 = mybir.dt.float32
BF16 = mybir.dt.bfloat16
I32 = mybir.dt.int32
U32 = mybir.dt.uint32
ALU = mybir.AluOpType
ACT = mybir.ActivationFunctionType
AX = mybir.AxisListType.X

NB = 16
NT = 32
NE = 8
NU = 71
NG = 18
ROW = 130
NOWHERE = 1 << 20
EPS = 1e-5

CW, _c = {}, 0
for _n, _w in [("ident", 128), ("dist", 512), ("upper", 128), ("e8", 256), ("unit", 72), ("head", 16)]:
    CW[_n] = (_c, _c + _w)
    _c += _w
CK = _c
AW, _c = {}, 0
for _n, _w in [("w0", 128), ("router", 8), ("rbias", 8), ("b0", 1)]:
    AW[_n] = (_c, _c + _w)
    _c += _w
AK = _c
DW, _c = {}, 0
for _n, _w in [("qkv", 128), ("wout", 128), ("wp1", 128), ("wp2", 8), ("bp1", 1), ("bp2", 8), ("temp", 16),
               ("bout", 128), ("wo", 128), ("bo", 128)]:
    DW[_n] = (_c, _c + _w)
    _c += _w
DK = _c
EK = 516


class Line:

    def __init__(self, sem):
        self.sem, self.count, self.steps, self.past = sem, 0, [], {}

    def wait(self, *toks):
        for t in toks:
            if t is None:
                continue
            if isinstance(t, list):
                self.wait(*t)
                continue
            sem, v = t
            if self.past.get(sem.name, 0) < v:
                self.past[sem.name] = v
                self.steps.append(lambda e, s=sem, n=v: e.wait_ge(s, n))

    def do(self, fn, *toks):
        self.wait(*toks)
        self.steps.append(fn)

    def tell(self, fn, *toks):
        self.wait(*toks)
        self.count += 1
        self.steps.append(lambda e, f=fn: f(e).then_inc(self.sem, 1))
        return (self.sem, self.count)

    def dma(self, fn, box, *toks):
        self.wait(*toks)
        box[1] += 16
        self.steps.append(lambda e, f=fn, s=box[0]: f(e).then_inc(s, 16))
        return (box[0], box[1])

    def run(self, e):
        for s in self.steps:
            s(e)


def mm(out, lhsT, rhs, start=True, stop=True):
    return lambda e: e.matmul(out, lhsT, rhs, start=start, stop=stop)


def tr(out, in_, ident):
    return lambda e: e.transpose(out, in_, ident)


def act(out, in_, func, bias=0.0, scale=1.0, accum=None):
    if accum is None:
        return lambda e: e.activation(out, in_, func, bias=bias, scale=scale)
    return lambda e: e.activation(out, in_, func, bias=bias, scale=scale, accum_out=accum)


def cp(out, in_):
    return lambda e: e.tensor_copy(out, in_)


def tt(out, a, b, op):
    return lambda e: e.tensor_tensor(out, a, b, op)


def ts(out, a, s1, s2=None, op0=ALU.mult, op1=None):
    if op1 is None:
        return lambda e: e.tensor_scalar(out, a, s1, None, op0)
    return lambda e: e.tensor_scalar(out, a, s1, s2, op0, op1)


def stt(out, a, s, b, op0, op1):
    return lambda e: e.scalar_tensor_tensor(out=out, in0=a, scalar=s, in1=b, op0=op0, op1=op1)


def ttr(out, a, b, op0, op1, init, accum):
    return lambda e: e.tensor_tensor_reduce(out, a, b, 1.0, init, op0, op1, accum)


def red(out, a, op, negate=False):
    if negate:
        return lambda e: e.tensor_reduce(out, a, AX, op, negate=True)
    return lambda e: e.tensor_reduce(out, a, AX, op)


def rcp(out, a):
    return lambda e: e.reciprocal(out, a)


def scan(out, a, b):
    return lambda e: e.tensor_tensor_scan(out, a, b, 0.0, ALU.mult, ALU.add)


def bc(ap, shape):
    return ap.unsqueeze(len(shape) - 1).broadcast_to(shape)


def program(nc, D, out):
    with ExitStack() as ctx:
        def sb(name, shape, dt=F32):
            return ctx.enter_context(nc.sbuf_tensor(name, shape, dt))

        def sem(name):
            return ctx.enter_context(nc.semaphore(name))

        X = sb("X", [128, NT, 128])
        XA = sb("XA", [128, NT, ROW])
        XB = sb("XB", [128, NT, ROW])
        XT = sb("XT", [128, NT * 128])
        FT = sb("FT", [128, NT * 128])
        F = sb("F", [128, NT, 128])
        S = sb("S", [128, NT, 128])
        SH = sb("SH", [128, NT, 128])
        C = sb("C", [128, CK])
        WA = sb("WA", [128, AK])
        WB = sb("WB", [128, 768])
        WE = sb("WE", [128, NE * 768])
        WD = sb("WD", [128, DK])
        DI = sb("DI", [128, 64], I32)
        E = sb("E", [128, 2, 2, 256])
        PR = sb("PR", [128, 2, 2, 256])
        PT = sb("PT", [128, 2, 2, 256])
        ST = sb("ST", [128, NT, 6])
        MV = sb("MV", [128, NT, 2])
        RS = sb("RS", [128, NT])
        NM = sb("NM", [128, NT])
        SU = sb("SU", [128, NT])
        EPSB = sb("EPSB", [128, 1])
        BFC = sb("BFC", [128, 3, 256], BF16)
        RW = sb("RW", [128, 12, 32])
        POS = sb("POS", [128, 2, NT], I32)
        NI = sb("NI", [128, 2, 8], I32)
        EU = sb("EU", [128, 72])
        EUI = sb("EUI", [128, 72], I32)
        ONE = sb("ONE", [128, 256])
        ZB = sb("ZB", [128, ROW])
        XS = sb("XS", [128, 4, 4, ROW])
        XG = sb("XG", [128, 2, 512])
        YS = sb("YS", [128, 8, 128])
        SG = FT[:, 0:1536].rearrange("p (a b) -> p a b", a=3)
        HH = FT[:, 1536:3072].rearrange("p (a b) -> p a b", a=3)
        XB_flat = XB[:, :, :].rearrange("p t r -> p (t r)")
        xs_flat = XS[:, :, :, :].rearrange("p a b c -> p (a b c)")
        xg_flat = XG[:, :, :].rearrange("p a b -> p (a b)")
        R8 = xs_flat[:, 0:2048].rearrange("p (a b) -> p a b", a=8)
        WS = xs_flat[:, 0:4 * EK].rearrange("p (a b) -> p a b", a=4)
        UC = xg_flat[:, 0:504].rearrange("p (u e) -> p u e", e=7)
        JK = xg_flat.rearrange("p (a b) -> p a b", a=4)
        PXP = YS[:, :, :].rearrange("p (a b) d -> p a b d", a=2)
        WE2 = WE[:, 0:4096]
        WC = XB_flat[:, 0:2048].rearrange("p (a b) -> p a b", a=4)
        YC = [T.rearrange("p (b q d) -> p b q d", b=8, q=4) for T in (XB_flat[:, 0:4096], WE2)]
        OT = WE[:, 4096:5120].rearrange("p (a b) -> p a b", a=2)
        LG = WE[:, 5120:5632].rearrange("p (c i h) -> p c i h", c=8, i=4)
        HB = WE[:, 5632:5888].rearrange("p (b h) -> p b h", h=16)
        MX = WE[:, 5888:5952].rearrange("p (c m) -> p c m", c=8)
        SM = sb("SM", [128, 8, 32])
        A1 = sb("A1", [128, 16])
        SEL = sb("SEL", [16, 6, 8])
        SELI = sb("SELI", [16, 8], U32)
        BO3 = sb("BO3", [128, 128])
        PS = [ctx.enter_context(nc.psum_tensor(f"PS{i}", [128, 512], F32)) for i in range(8)]

        xs = nc.dram_tensor("xs_scratch", [NG * 4 * 128, ROW], F32, kind="Internal").ap()
        yc = nc.dram_tensor("yc_scratch", [NB * 128 * 4, 128], F32, kind="Internal").ap()

        def c_(n):
            return C[:, CW[n][0]:CW[n][1]]

        def a_(n):
            return WA[:, AW[n][0]:AW[n][1]]

        def d_(n):
            return WD[:, DW[n][0]:DW[n][1]]

        ident = c_("ident")
        pe, dve, sc, po, sp = (Line(sem(n)) for n in ("pe", "dve", "act", "pool", "sp"))
        box = {}

        def dsem(name):
            if name not in box:
                box[name] = [sem("d_" + name), 0]
            return box[name]

        def load(dst, src, name, *toks):
            return sp.dma(lambda e: e.dma_start(dst, src), dsem(name), *toks)

        def tile(T, t, n=1):
            return T[:, t * 128:(t + n) * 128]

        free = [None] * 8

        x_in = []

        def load_x(c):
            for b in (2 * c, 2 * c + 1):
                tok = load(X[:, 2 * b:2 * b + 2, :].rearrange("p i d -> p (i d)"),
                           D["x"][b].rearrange("(p i) d -> p (i d)", i=2), f"x{c}")
            x_in.append(tok)

        load_x(0)
        l_id = load(C[:, 0:128], D["consts"][:, 0:128], "id")
        l_wa = load(WA[:, :], D["wa"], "wa")
        load_x(1)
        for c in range(2, 8):
            load_x(c)
        l_c = load(C[:, 128:CK], D["consts"][:, 128:CK], "c")
        l_di = load(DI[:, :], D["dest"], "di")
        z1 = po.tell(lambda e: e.memset(ZB[:, :], 0.0))
        z2 = po.tell(lambda e: e.memset(ZB[:, 128:129].bitcast(I32), NOWHERE), z1)
        l_fill = load(xs.rearrange("(u p) r -> p u r", p=128), ZB[:, :].unsqueeze(1).broadcast_to([128, NG * 4, ROW]),
                      "fill", z2, x_in)
        l_wb = load(WB[:, :], D["wb"], "wb")
        l_we = load(WE[:, :], D["we"], "we")
        l_wd = load(WD[:, :], D["wd"], "wd")

        k_eps = po.tell(lambda e: e.memset(EPSB[:, :], EPS))
        k_one = po.tell(lambda e: e.memset(ONE[:, :], 1.0))
        k_bf1 = po.tell(lambda e: e.memset(BFC[:, 1, :], 1.0))

        def stats(T, t0, n, *toks):
            def one(t):
                return lambda e: e.bn_stats(ST[:, t, :], T[:, t, :])

            def two_(t):
                return lambda e: e.bn_aggr(MV[:, t, :], ST[:, t, :])
            a = [dve.tell(one(t), *toks) for t in range(t0, t0 + n)]
            return [dve.tell(two_(t), a[t - t0]) for t in range(t0, t0 + n)][-1]

        xt_done, xa_done, xb_done, sd_done = [], [], [], []

        def spread_in(c):
            t0 = 4 * c
            mv = stats(X, t0, 4, x_in[c])
            sd_done.append(sc.tell(act(RS[:, t0:t0 + 4], MV[:, t0:t0 + 4, 1], ACT.Sqrt, bias=EPSB[:, :]), mv, k_eps))

        def norm_in(c):
            t0 = 4 * c
            rs = dve.tell(rcp(RS[:, t0:t0 + 4], RS[:, t0:t0 + 4]), sd_done[c])
            for t in range(t0, t0 + 4):
                xa = dve.tell(ts(XA[:, t, 0:128], X[:, t, :], MV[:, t, 0:1], RS[:, t:t + 1], ALU.subtract, ALU.mult), rs)
            xa_done.append(xa)

        def turn_in(c):
            k = c % 2
            for j in range(4):
                tok = pe.tell(tr(PS[k][:, j * 128:(j + 1) * 128], XA[:, 4 * c + j, 0:128], ident), xa_done[c], l_id, free[k])
            free[k] = sc.tell(act(tile(XT, 4 * c, 4), PS[k][:, :], ACT.Copy), tok)
            xt_done.append(free[k])

        ft_done, f_done = [], []

        def logits(c):
            for t in range(4 * c, 4 * c + 4):
                tok = pe.tell(mm(PS[2][:, 8 * t:8 * t + 8], tile(XT, t), a_("router")), xt_done[c], l_wa)
            return tok

        def project(c):
            k = 3 + c % 2
            ft = pe.tell(mm(PS[k][:, :], a_("w0"), tile(XT, 4 * c, 4)), free[k])
            free[k] = sc.tell(act(tile(FT, 4 * c, 4), PS[k][:, :], ACT.Identity, bias=a_("b0")), ft, l_wa)
            ft_done.append(free[k])

        def turn_f(c):
            k = 5 + c % 2
            for j in range(4):
                tok = pe.tell(tr(PS[k][:, j * 128:(j + 1) * 128], tile(FT, 4 * c + j), ident), ft_done[c], free[k])
            free[k] = sc.tell(act(F[:, 4 * c:4 * c + 4, :], PS[k][:, :].rearrange("p (t d) -> p t d", d=128), ACT.Copy), tok)
            f_done.append(free[k])

        EARLY, MID = 3, 6
        spread_in(0)
        spread_in(1)
        for i in range(8 + 2):
            if i + 2 < 8:
                spread_in(i + 2)
            if i < 8:
                norm_in(i)
            if 1 <= i < 9:
                turn_in(i - 1)
            if 2 <= i:
                lg = logits(i - 2)
                if i - 2 < EARLY:
                    project(i - 2)
            if 3 <= i < EARLY + 2:
                turn_f(i - 3)
        for c in range(8):
            xb_done.append(po.tell(cp(XB[:, 4 * c:4 * c + 4, 0:128], XA[:, 4 * c:4 * c + 4, 0:128]), xa_done[c]))

        def et(ap):
            return ap.rearrange("p (e t) -> p e t", e=NE)

        def te(ap):
            return ap.rearrange("p (e t) -> p t e", e=NE)

        def over_e(ap):
            return ap.unsqueeze(1).broadcast_to([128, NE, NT])

        lgs, prob, eq, cand, oh1, oh2, ex, pos = (R8[:, i, :] for i in range(8))
        m1, m2, i1, i2, rw, w1, w2 = (RW[:, i, :] for i in range(7))
        base = RW[:, 8:12, :].rearrange("p a b -> p (a b)")
        pad, cum, corr = (base[:, 8 * i:8 * i + 8] for i in range(3))

        upper = dve.tell(cp(BFC[:, 0, 0:128], c_("upper")), l_c)
        q = dve.tell(tt(et(lgs), PS[2][:, 0:256].rearrange("p (t e) -> p e t", e=NE), bc(a_("rbias"), [128, NE, NT]),
                        ALU.add), lg, l_wa)
        free[2] = q
        q = sc.tell(act(prob, lgs, ACT.Sigmoid), q)
        for c in range(EARLY, MID):
            project(c)
            if c > 0:
                turn_f(c - 1)
        dve.do(cp(XA[:, :, 128].bitcast(I32), DI[:, 0:32]), l_di, xa_done)
        cols = dve.tell(cp(XB[:, :, 128].bitcast(I32), DI[:, 32:64]))

        def top(p, m, i, oh, tok):
            tok = dve.tell(red(m, te(p), ALU.max), tok)
            tok = dve.tell(tt(et(eq), et(p), over_e(m), ALU.is_equal), tok)
            tok = dve.tell(tt(cand, eq, c_("e8"), ALU.mult), tok)
            tok = dve.tell(red(i, te(cand), ALU.min), tok)
            return dve.tell(tt(et(oh), et(c_("e8")), over_e(i), ALU.is_equal), tok)

        q = top(prob, m1, i1, oh1, q)
        q = dve.tell(stt(lgs, oh1, -2.0, prob, ALU.mult, ALU.add), q)
        q = top(lgs, m2, i2, oh2, q)
        mask = dve.tell(tt(BFC[:, 2, :], oh1, oh2, ALU.add), q)
        r1 = pe.tell(mm(PS[7][:, 0:256], BFC[:, 0, 0:128], BFC[:, 2, :]), mask, upper, free[7])
        r2 = pe.tell(mm(PS[7][:, 256:512], BFC[:, 1, 0:128], BFC[:, 2, :]), k_bf1)
        for c in range(MID, 8):
            project(c)
            turn_f(c - 1)
        turn_f(7)
        within, total = PS[7][:, 0:256], PS[7][:, 256:512]
        w = dve.tell(tt(rw, m1, m2, ALU.add))
        w = dve.tell(rcp(rw, rw), w)
        dve.do(tt(XA[:, :, 129], m1, rw, ALU.mult), w, *xa_done)
        cols = dve.tell(tt(XB[:, :, 129], m2, rw, ALU.mult))
        q = dve.tell(scan(cand, ONE[:, :], total), r2, k_one)
        q = dve.tell(tt(ex, cand, total, ALU.subtract), q)
        summed = q
        q = dve.tell(stt(NI[:, 0, :], et(cand)[:, :, 31], 127.0, et(ex)[:, :, 0], ALU.add, ALU.subtract), q)
        free[7] = dve.tell(tt(pos, within, ex, ALU.add), summed)
        q = dve.tell(ts(NI[:, 1, :], NI[:, 0, :], -128, None, ALU.bitwise_and), q)
        q = dve.tell(cp(pad, NI[:, 1, :]), q)
        cq = dve.tell(scan(cum, ONE[:, 0:8], pad), q)
        q = dve.tell(tt(corr, cum, pad, ALU.subtract), cq)
        q = dve.tell(tt(corr, corr, et(ex)[:, :, 0], ALU.subtract), q)
        q = dve.tell(tt(et(pos), et(pos), bc(corr, [128, NE, NT]), ALU.add), q, free[7])
        q1 = dve.tell(tt(oh1, oh1, pos, ALU.mult), q)
        q2 = dve.tell(tt(oh2, oh2, pos, ALU.mult), q)
        dve.do(red(w1, te(oh1), ALU.add), q1)
        q = dve.tell(red(w2, te(oh2), ALU.add), q2)
        places = dve.tell(cp(POS[:, :, :], RW[:, 5:7, :]), q)
        q = dve.tell(tt(UC[:, :, :], bc(c_("unit"), [128, 72, 7]), cum[:, 0:7].unsqueeze(1).broadcast_to([128, 72, 7]),
                        ALU.is_ge), cq)
        q = dve.tell(red(EU[:, :], UC[:, :, :], ALU.add), q)
        experts = dve.tell(ts(EUI[:, :], EU[:, :], 768.0, None, ALU.mult), q)

        def scatter(dst, idx, src, name, bound, *toks):
            return po.dma(lambda e: e.indirect_dma_start(
                out=dst, out_offset=bass.IndirectOffsetOnAxis(ap=idx, axis=0), in_=src, in_offset=None,
                bounds_check=bound, oob_is_err=False), dsem(name), *toks)

        po.wait(places, cols, l_fill, *xb_done)
        for t in range(NT):
            scatter(xs, POS[:, 0, t:t + 1], XA[:, t, :], "disp", NG * 4 * 128 - 1)
            dispatched = scatter(xs, POS[:, 1, t:t + 1], XB[:, t, :], "disp", NG * 4 * 128 - 1)

        sc_done, ex_done, pt_done = {}, {}, {}
        pv_read, s_done = {}, {}

        def scores(b):
            k = b % 2
            for i in range(2):
                tok = pe.tell(mm(PS[k][:, i * 256:(i + 1) * 256], tile(FT, 2 * b + i), tile(FT, 2 * b, 2)),
                              ft_done[b // 2], free[k])
            for i in range(2):
                t = 2 * b + i
                e1 = dve.tell(ttr(E[:, k, i, :], PS[k][:, i * 256:(i + 1) * 256],
                                  c_("dist")[:, i * 256:(i + 1) * 256], ALU.add, ALU.max, -3.0e38, RW[:, 7, t:t + 1]),
                              tok, l_c, ex_done.get(b - 2))
            free[k] = e1
            nm = dve.tell(ts(NM[:, 2 * b:2 * b + 2], RW[:, 7, 2 * b:2 * b + 2], -1.0), e1)
            for i in range(2):
                t = 2 * b + i
                tok = sc.tell(act(PR[:, k, i, :], E[:, k, i, :], ACT.Exp, bias=NM[:, t:t + 1], accum=SU[:, t:t + 1]),
                              nm, pt_done.get(b - 2))
            ex_done[b] = tok
            sc_done[b] = dve.tell(rcp(SU[:, 2 * b:2 * b + 2], SU[:, 2 * b:2 * b + 2]), tok)

        def turn_p(b):
            k, kb = 3 + b % 2, b % 2
            for j in range(2):
                for i in range(2):
                    tok = pe.tell(tr(PS[k][:, j * 256 + i * 128:j * 256 + (i + 1) * 128],
                                     PR[:, kb, i, j * 128:(j + 1) * 128], ident), ex_done[b], free[k])
            pt_done[b] = tok
            free[k] = dve.tell(cp(PT[:, kb, :, :], PS[k][:, :].rearrange("p (j i) -> p j i", j=2)), tok, pv_read.get(b - 2))

        def mix(b):
            k, kb = 5 + b % 2, b % 2
            for i in range(2):
                for j in range(2):
                    tok = pe.tell(mm(PS[k][:, i * 128:(i + 1) * 128], PT[:, kb, j, i * 128:(i + 1) * 128],
                                     F[:, 2 * b + j, :], start=j == 0, stop=j == 1),
                                  free[3 + b % 2], free[k], f_done[b // 2])
            pv_read[b] = tok
            for i in range(2):
                t = 2 * b + i
                free[k] = sc.tell(act(S[:, t, :], PS[k][:, i * 128:(i + 1) * 128], ACT.Copy, scale=SU[:, t:t + 1]),
                                  tok, sc_done[b])
            s_done[b] = free[k]

        for i in range(NB + 2):
            if i < NB:
                scores(i)
            if 1 <= i < NB + 1:
                turn_p(i - 1)
            if i >= 2:
                mix(i - 2)

        h_done, h_read, sg_read, ehr, sh_done = {}, {}, {}, {}, {}

        def up(j):
            c, f = divmod(j, 2)
            k = 2 * (j % 2)
            g = pe.tell(mm(PS[k][:, :], WB[:, f * 128:(f + 1) * 128], tile(XT, 4 * c, 4)), l_wb, free[k])
            u = pe.tell(mm(PS[k + 1][:, :], WB[:, 256 + f * 128:256 + (f + 1) * 128], tile(XT, 4 * c, 4)), free[k + 1])
            free[k] = sc.tell(act(SG[:, j % 3, :], PS[k][:, :], ACT.Silu), g, sg_read.get(j - 3), sc_done[NB - 1],
                              sg_read.get(("e", NU - 1)))
            free[k + 1] = dve.tell(tt(HH[:, j % 3, :], SG[:, j % 3, :], PS[k + 1][:, :], ALU.mult), u, free[k],
                                   h_read.get(j - 3), ehr.get(NU - 1))
            sg_read[j] = h_done[j] = free[k + 1]

        def down(c):
            k = 4 + c % 2
            for t in range(4):
                for f in range(2):
                    tok = pe.tell(mm(PS[k][:, t * 128:(t + 1) * 128], HH[:, (2 * c + f) % 3, t * 128:(t + 1) * 128],
                                     WB[:, 512 + f * 128:512 + (f + 1) * 128], start=f == 0, stop=f == 1),
                                  h_done[2 * c + 1], free[k])
            h_read[2 * c] = h_read[2 * c + 1] = tok
            free[k] = sc.tell(act(SH[:, 4 * c:4 * c + 4, :], PS[k][:, :].rearrange("p (t d) -> p t d", d=128), ACT.Copy), tok)
            sh_done[c] = free[k]

        def shared(c0, c1):
            for j in range(2 * c0, 2 * c1):
                up(j)
                if j % 2 == 0 and j > 2 * c0:
                    down(j // 2 - 1)
            down(c1 - 1)

        LATE = 5
        shared(0, LATE)
        JL = 2 * LATE - 1

        xs_in, xs_read, xg_done, xg_read = {}, {}, {}, {}
        eh_done, wc_done, wc_read, y_out = {}, {}, {}, {}
        ys_done = {}
        nu = [min(4, NU - 4 * g) for g in range(NG)]

        def fetch(g):
            n = nu[g]
            xs_in[g] = load(XS[:, g % 4, 0:n, :], xs[g * 512:g * 512 + n * 128, :].rearrange("(u p) r -> p u r", p=128),
                            f"xs{g % 4}", dispatched, xs_read.get(g - 4), y_out.get(4 * (g - 4) + 3))

        def turn_x(g):
            for j in range(nu[g]):
                tok = pe.tell(tr(PS[6][:, j * 128:(j + 1) * 128], XS[:, g % 4, j, 0:128], ident), xs_in[g], free[6])
            xs_read[g] = tok
            free[6] = sc.tell(act(XG[:, g % 2, 0:nu[g] * 128], PS[6][:, 0:nu[g] * 128], ACT.Copy), tok, xg_read.get(g - 2))
            xg_done[g] = free[6]

        reg = {}

        def pick(u):
            def f(e):
                reg[u] = e.value_load(EUI[0:1, u:u + 1], min_val=0, max_val=7 * 768)
            pe.do(f, experts, l_we)

        def choose(u):
            def f(e):
                r = e.value_load(EUI[0:1, u:u + 1], min_val=0, max_val=7 * 768)
                return e.tensor_copy(WC[:, u % 4, :], WE[:, bass.ds(r, 512)])
            wc_done[u] = dve.tell(f, experts, l_we, dispatched, wc_read.get(u - 4))

        def gate_up(u):
            g, j = divmod(u, 4)
            k = u % 3
            pick(u)
            for f in range(4):
                tok = pe.tell(mm(PS[k][:, f * 128:(f + 1) * 128], WC[:, u % 4, f * 128:(f + 1) * 128],
                                 XG[:, g % 2, j * 128:(j + 1) * 128]), xg_done[g], wc_done[u], free[k])
            wc_read[u] = tok
            if j == nu[g] - 1:
                xg_read[g] = tok
            a = sc.tell(act(SG[:, u % 3, 0:256], PS[k][:, 0:256], ACT.Silu), tok, sg_read.get(("e", u - 3)), sg_read[JL])
            free[k] = dve.tell(tt(HH[:, u % 3, 0:256], SG[:, u % 3, 0:256], PS[k][:, 256:512], ALU.mult), a,
                               ehr.get(u - 3), h_read[JL])
            sg_read[("e", u)] = eh_done[u] = free[k]

        def down_e(u):
            g, j = divmod(u, 4)
            k = (5, 7)[u % 2]
            for f in range(2):
                tok = pe.tell(lambda e, f=f: e.matmul(PS[k][:, 0:128], HH[:, u % 3, f * 128:(f + 1) * 128],
                                                      WE[:, bass.ds(reg[u] + (512 + f * 128), 128)],
                                                      start=f == 0, stop=f == 1), eh_done[u], free[k])
            ehr[u] = tok
            free[k] = sc.tell(act(YS[:, u % 8, :], PS[k][:, 0:128], ACT.Copy, scale=XS[:, g % 4, j, 129:130]), tok,
                              y_out.get(u - 8))
            ys_done[u] = free[k]
            y_out[u] = scatter(yc, XS[:, g % 4, j, 128:129].bitcast(U32), YS[:, u % 8, :], f"y{u % 8}", NB * 128 * 4 - 1,
                               ys_done[u])

        for g in range(3):
            fetch(g)
        turn_x(0)
        choose(0)
        choose(1)
        for u in range(NU + 2):
            if u < NU:
                if u + 2 < NU:
                    choose(u + 2)
                gate_up(u)
                if u % 4 == 2 and u // 4 + 1 < NG:
                    turn_x(u // 4 + 1)
                if u % 4 == 3 and u // 4 + 3 < NG:
                    fetch(u // 4 + 3)
            if u >= 2:
                down_e(u - 2)
        routed = [y_out[u] for u in range(NU - 8, NU)]

        NC = 8
        WT, W2, XNB = FT, WE2, SH
        yin, added, gated, rooted = {}, {}, {}, {}
        x1_done, x1_mid, xn_done, xt1_done = {}, {}, {}, {}
        bo3 = dve.tell(ts(BO3[:, :], d_("bo"), 0.3), l_wd)
        half_b = dve.tell(ts(d_("bout"), d_("bout"), 0.5), l_wd)

        def four(T, c):
            return T[:, 4 * c:4 * c + 4, 0:128]

        def collect(c):
            for b in (2 * c, 2 * c + 1):
                yin[c] = load(YC[b // 8][:, b % 8, :, :].rearrange("p q d -> p (q d)"),
                              yc.rearrange("(b p q) d -> b p (q d)", b=NB, q=4)[b], f"yt{c}", routed, dispatched)

        def results(c):
            y = YC[c // 4][:, 2 * (c % 4):2 * (c % 4) + 2, :, :].rearrange("p b (i s) d -> p b i s d", s=2)
            return y[:, :, :, 0, :], y[:, :, :, 1, :]

        def end0(c):
            y = results(c)
            a = dve.tell(tt(four(F, c).rearrange("p (b i) d -> p b i d", b=2), y[0], y[1], ALU.add), yin[c],
                         pv_read[NB - 1])
            added[c] = dve.tell(tt(four(SH, c), four(SH, c), four(F, c), ALU.add), a, sh_done[c])
            gated[c] = sc.tell(act(four(F, c), four(SH, c), ACT.Silu), added[c])

        def down_late(c):
            k = c - LATE + 4
            for t in range(4):
                for f in range(2):
                    h_read[2 * c] = h_read[2 * c + 1] = pe.tell(
                        mm(PS[k][:, t * 128:(t + 1) * 128], HH[:, (2 * c + f) % 3, t * 128:(t + 1) * 128],
                           WB[:, 512 + f * 128:512 + (f + 1) * 128], start=t == 0 and f == 0, stop=False),
                        h_done[2 * c + 1], free[k])

        def end0_late(c):
            k = c - LATE + 4
            for s in range(2):
                tok = pe.tell(mm(PS[k][:, :], ident, results(c)[s], start=False, stop=s == 1), yin[c])
            added[c] = tok
            free[k] = gated[c] = sc.tell(act(four(F, c), PS[k][:, :].rearrange("p (t d) -> p t d", d=128), ACT.Silu),
                                         tok, pv_read[NB - 1])

        def rest0(c):
            m = po.tell(tt(four(F, c), four(F, c), four(S, c), ALU.mult), gated[c], s_done[NB - 1])
            if c % 2:
                m = po.tell(tt(four(X, c), four(X, c), four(F, c), ALU.add), m)
            x1_done[c] = m

        def stats1(c):
            if c % 2 == 0:
                x1_done[c] = dve.tell(tt(four(X, c), four(X, c), four(F, c), ALU.add), x1_done[c])
            x1_mid[c] = stats(X, 4 * c, 4, x1_done[c])

        def root1(c):
            t = slice(4 * c, 4 * c + 4)
            rooted[c] = sc.tell(act(RS[:, t], MV[:, t, 1], ACT.Sqrt, bias=EPSB[:, :]), x1_mid[c])

        def norm1(c):
            r = slice(4 * c, 4 * c + 4)
            rs = dve.tell(rcp(RS[:, r], RS[:, r]), rooted[c])
            for t in range(4 * c, 4 * c + 4):
                xn_done[c] = dve.tell(ts(XA[:, t, 0:128], X[:, t, :], MV[:, t, 0:1], RS[:, t:t + 1], ALU.subtract,
                                         ALU.mult), rs)

        def turn1(c):
            k = c % 2
            for i in range(4):
                tok = pe.tell(tr(PS[k][:, i * 128:(i + 1) * 128], XA[:, 4 * c + i, 0:128], ident), xn_done[c], free[k])
            free[k] = sc.tell(act(tile(XT, 4 * c, 4), PS[k][:, :], ACT.Copy), tok)
            xt1_done[c] = free[k]

        N2, RN, DOT, SPI = (SM[:, i, 0:16] for i in range(4))
        HM = SM[:, 4, 0:16]
        hm = dve.tell(tt(HM, c_("head"), d_("temp"), ALU.mult), l_wd, l_c)
        w_done, hb_done, lg_done, px_done, px_read, ot_done, ot_read, s1_done, w2_read = ({} for _ in range(9))
        heads_in, heads_out, n2_done, heads_ps, pi_read, proj_ps = {}, {}, {}, {}, {}, {}

        def w2v(b):
            return W2[:, b * 256:(b + 1) * 256]

        def proj(c):
            k = 2 + c % 2
            tok = pe.tell(mm(PS[k][:, :], d_("qkv"), tile(XT, 4 * c, 4)), xt1_done[c], l_wd, free[k])
            proj_ps[c] = tok

        def squares(c):
            k, tok = 2 + c % 2, proj_ps[c]
            for h in range(2):
                b = 2 * c + h
                n2 = sc.tell(act(w2v(b), PS[k][:, h * 256:(h + 1) * 256], ACT.Square, accum=N2[:, b:b + 1]),
                             tok, [added[i] for i in range(4, NC)])
            free[k] = sc.tell(act(tile(WT, 4 * c, 4), PS[k][:, :], ACT.Copy), h_read[15])
            w_done[c] = free[k]
            n2_done[c] = n2

        def weigh(c):
            bb, n2 = slice(2 * c, 2 * c + 2), n2_done[c]
            r = dve.tell(ts(RN[:, bb], N2[:, bb], 1e-24, None, ALU.max), n2)
            r = dve.tell(rcp(RN[:, bb], RN[:, bb]), r)
            hb_done[c] = dve.tell(tt(HB[:, bb, :], HM.unsqueeze(1).broadcast_to([128, 2, 16]),
                                     bc(RN[:, bb], [128, 2, 16]), ALU.mult), r, hm)

        def heads(c):
            k = 4 + c % 3
            for i in range(4):
                b = 2 * c + i // 2
                tok = pe.tell(mm(PS[k][:, i * 16:(i + 1) * 16], w2v(b)[:, i % 2 * 128:(i % 2 + 1) * 128], HB[:, b, :]),
                              hb_done[c], free[k])
            heads_ps[c] = tok

        def center(c):
            k = 4 + c % 3
            lg = PS[k][:, 0:64].rearrange("p (i h) -> p i h", i=4)
            m = dve.tell(red(MX[:, c, 0:4], lg, ALU.max), heads_ps[c])
            free[k] = dve.tell(tt(LG[:, c, :, :], lg, bc(MX[:, c, 0:4], [128, 4, 16]), ALU.subtract), m)
            heads_in[c] = free[k]

        def soft(c):
            heads_out[c] = sc.tell(act(LG[:, c, :, :], LG[:, c, :, :], ACT.Exp), heads_in[c])

        def share(c):
            m = dve.tell(red(MX[:, c, 4:8], LG[:, c, :, :], ALU.add), heads_out[c])
            m = dve.tell(rcp(MX[:, c, 4:8], MX[:, c, 4:8]), m)
            px_done[c] = dve.tell(tt(PXP[:, c % 2, :, :].rearrange("p i (h d) -> p i h d", d=8),
                                     bc(LG[:, c, :, :], [128, 4, 16, 8]),
                                     MX[:, c, 4:8].unsqueeze(2).unsqueeze(3).broadcast_to([128, 4, 16, 8]), ALU.mult),
                                  m, px_read.get(c - 2))

        def spread(c):
            k, v = c % 2, PR[:, c % 2, :, :]
            for i in range(4):
                tok = pe.tell(tr(PS[k][:, i * 128:(i + 1) * 128], PXP[:, c % 2, i, :], ident), px_done[c], free[k])
            px_read[c] = tok
            bb = slice(2 * c, 2 * c + 2)
            for h in range(2):
                b = 2 * c + h
                free[k] = sc.tell(act(v[:, h, :], PS[k][:, h * 256:(h + 1) * 256], ACT.Copy, accum=SPI[:, b:b + 1]), tok,
                                  pi_read.get(c - 2))
            d = []
            for h in range(2):
                b = 2 * c + h
                d.append(dve.tell(ttr(JK[:, b % 4, :], v[:, h, :], w2v(b), ALU.mult, ALU.add, 0.0, DOT[:, b:b + 1]), free[k]))
            q = dve.tell(ts(SPI[:, bb], SPI[:, bb], 1e-8, None, ALU.add))
            q = dve.tell(rcp(SPI[:, bb], SPI[:, bb]), q)
            q = dve.tell(tt(DOT[:, bb], DOT[:, bb], SPI[:, bb], ALU.mult), q, d)
            q = dve.tell(ts(DOT[:, bb], DOT[:, bb], 1.0, None, ALU.add), q)
            q = dve.tell(rcp(DOT[:, bb], DOT[:, bb]), q)
            for h in range(2):
                b = 2 * c + h
                pi_read[c] = dve.tell(stt(OT[:, c % 2, h * 256:(h + 1) * 256], v[:, h, :], DOT[:, b:b + 1],
                                          tile(WT, 2 * b, 2), ALU.mult, ALU.mult),
                                      q, w_done[c], ot_read.get(c - 2))
            ot_done[c] = pi_read[c]

        def out1(c):
            k = 7
            for i in range(4):
                tok = pe.tell(mm(PS[k][:, i * 128:(i + 1) * 128], OT[:, c % 2, i * 128:(i + 1) * 128], d_("wout")),
                              ot_done[c], free[k])
            ot_read[c] = tok
            free[k] = dve.tell(stt(four(S, c), PS[k][:, :].rearrange("p (i d) -> p i d", d=128), -0.5,
                                   d_("bout").unsqueeze(1).broadcast_to([128, 4, 128]), ALU.mult, ALU.add), tok, half_b)
            s1_done[c] = free[k]

        for c in range(NC):
            collect(c)
        for j in range(2 * LATE, 16):
            up(j)
            if j % 2 == 0 and j > 2 * LATE:
                down_late(j // 2 - 1)
            if j >= 13:
                end0(j - 13)
                rest0(j - 13)
        down_late(7)
        for c in range(3, LATE):
            end0(c)
            rest0(c)
        for c in range(LATE, NC):
            end0_late(c)
            rest0(c)
        AHEAD = 4
        for c in range(AHEAD):
            stats1(c)
            root1(c)
        for i in range(NC + 1):
            if 1 <= i and i + AHEAD - 1 < NC:
                stats1(i + AHEAD - 1)
                root1(i + AHEAD - 1)
            if 1 <= i:
                norm1(i - 1)
            if 4 <= i:
                weigh(i - 4)
            if 5 <= i:
                center(i - 5)
            if 1 <= i:
                turn1(i - 1)
            if 2 <= i:
                proj(i - 2)
            if 2 <= i < NC:
                squares(i - 2)
            if 4 <= i < NC:
                heads(i - 4)
        tok = pe.tell(mm(PS[7][:, 0:16], d_("wp1"), XT[:, 255::256]), l_wd, [xt1_done[c] for c in range(NC)], free[7])
        a1 = sc.tell(act(A1[:, :], PS[7][:, 0:16], ACT.Gelu, bias=d_("bp1")), tok)
        squares(6)
        heads(4)
        proj(7)
        squares(7)
        weigh(5)
        heads(5)
        center(4)
        tok = pe.tell(mm(PS[7][0:16, 0:8], A1[:, :], d_("wp2")), a1)
        lt = SEL[:, 0, :]
        tok = dve.tell(tt(lt, PS[7][0:16, 0:8], d_("bp2")[0:16, :], ALU.add), tok)
        free[7] = tok
        tok = dve.tell(red(SEL[:, 1, 0:1], lt, ALU.max, negate=True), tok)
        tok = sc.tell(act(SEL[:, 2, :], lt, ACT.Exp, bias=SEL[:, 1, 0:1], accum=SEL[:, 3, 0:1]), tok)
        weigh(6)
        heads(6)
        weigh(7)
        center(5)
        heads(7)
        early = 6
        for c in range(early):
            soft(c)
        tok = dve.tell(rcp(SEL[:, 3, 0:1], SEL[:, 3, 0:1]), tok)
        tok = dve.tell(ts(SEL[:, 2, :], SEL[:, 2, :], SEL[:, 3, 0:1]), tok)
        tok = dve.tell(lambda e: e.max(SEL[:, 4, :], SEL[:, 2, :]), tok)
        chosen = dve.tell(lambda e: e.max_index(SELI[:, :], SEL[:, 4, :], SEL[:, 2, :]), tok)
        center(6)
        center(7)
        ws_in, ws_read = {}, {}

        def expert1(b):
            s = b % 4

            def f(e):
                v = e.value_load(SELI[b:b + 1, 0:1], min_val=0, max_val=7)
                return e.dma_start(WS[:, s, :], D["w1"][bass.ds(v, 1)].rearrange("o p k -> p (o k)"))
            ws_in[b] = sp.dma(f, dsem(f"ws{s}"), chosen, routed, ws_read.get(b - 4))

        for b in range(4):
            expert1(b)

        H1 = E
        RT = PT
        xnb_done, h1_done, h1_read, rt_done, rt_read, t_done = {}, {}, {}, {}, {}, {}
        for c in range(NC):
            xnb_done[c] = po.tell(tt(four(XNB, c), four(XA, c), BO3[:, :].unsqueeze(1).broadcast_to([128, 4, 128]), ALU.add),
                                  xn_done[c], bo3)

        def ff_up(b):
            k, s = 2 + b % 2, b % 4
            for f in range(2):
                tok = pe.tell(mm(PS[k][:, f * 256:(f + 1) * 256], WS[:, s, f * 128:(f + 1) * 128], tile(XT, 2 * b, 2)),
                              ws_in[b], free[k])
            for f in range(2):
                free[k] = sc.tell(act(H1[:, b % 2, f, :], PS[k][:, f * 256:(f + 1) * 256], ACT.Gelu,
                                      bias=WS[:, s, 512 + f:513 + f]), tok, h1_read.get(b - 2))
            h1_done[b] = free[k]

        def ff_down(b):
            k, s = 4, b % 4
            for f in range(2):
                tok = pe.tell(mm(PS[k][:, 0:256], WS[:, s, 256 + f * 128:256 + (f + 1) * 128], H1[:, b % 2, f, :],
                                 start=f == 0, stop=f == 1), h1_done[b], free[k])
            h1_read[b] = tok
            free[k] = sc.tell(act(RT[:, b % 2, 0, :], PS[k][:, 0:256], ACT.Identity, bias=WS[:, s, 514:515]), tok,
                              rt_read.get(b - 2))
            rt_done[b] = ws_read[b] = free[k]
            if b + 4 < NB:
                expert1(b + 4)

        def ff_out(b):
            k, h, c = 6 if b == NB - 1 else 5, b % 2, b // 2
            for i in range(2):
                tok = pe.tell(mm(PS[k][:, (2 * h + i) * 128:(2 * h + i + 1) * 128], RT[:, b % 2, 0, i * 128:(i + 1) * 128],
                                 d_("wo")), rt_done[b], free[k])
            rt_read[b] = tok
            v = [PS[k][:, 256 * i:256 * i + 256].rearrange("p (i d) -> p i d", i=2) for i in range(2)]
            if c == NC - 1:
                t_done[b] = dve.tell(stt(XNB[:, 2 * b:2 * b + 2, :], v[h], 0.3, XNB[:, 2 * b:2 * b + 2, :], ALU.mult, ALU.add),
                                     tok, xnb_done[c])
                free[k] = t_done[b]
            elif h == 1:
                free[k] = dve.tell(stt(four(XNB, c), PS[k][:, :].rearrange("p (i d) -> p i d", i=4), 0.3,
                                       four(XNB, c), ALU.mult, ALU.add), tok, xnb_done[c])
                t_done[b - 1] = t_done[b] = free[k]

        stored, finished = [], []

        def end1(b, n, last):
            r = slice(2 * b, 2 * b + 2 * n)
            g = sc.tell(act(F[:, r, :], XNB[:, r, :], ACT.Tanh, scale=0.5), t_done[b])
            g = dve.tell(stt(F[:, r, :], F[:, r, :], 1.0, XNB[:, r, :], ALU.add, ALU.mult), g)
            e = dve if last else po
            m = e.tell(tt(F[:, r, :], F[:, r, :], S[:, r, :], ALU.mult), g, s1_done[b // 2])
            a = e.tell(tt(X[:, r, :], X[:, r, :], F[:, r, :], ALU.add), m)
            for i in range(b, b + n):
                finished.append((i, a))

        def store():
            while finished:
                i, a = finished.pop(0)
                stored.append(load(out[i].rearrange("(p i) d -> p (i d)", i=2),
                                   X[:, 2 * i:2 * i + 2, :].rearrange("p i d -> p (i d)"), "out", a))

        share(0)
        share(1)
        for c in range(early, NC):
            soft(c)
        for b in range(NB + 3):
            if b % 2 == 0 and b < NB:
                c = b // 2
                spread(c)
                if c + 2 < NC:
                    share(c + 2)
            if b < NB:
                ff_up(b)
            if b % 2 == 1 and b < NB:
                out1(b // 2)
            if 1 <= b < NB + 1:
                ff_down(b - 1)
            if 2 <= b < NB + 2:
                ff_out(b - 2)
            if b >= 4 and b % 2 == 0 and b < NB + 2:
                store()
                end1(b - 4, 2, False)
            if b >= NB + 1:
                end1(b - 3, 1, True)
                store()
        sp.wait(stored[-1], dispatched, l_fill, [y_out[u] for u in range(NU)])

        block = ctx.enter_context(nc.Block())

        @block.sync
        def _(e):
            sp.run(e)

        @block.tensor
        def _(e):
            pe.run(e)

        @block.vector
        def _(e):
            dve.run(e)

        @block.scalar
        def _(e):
            sc.run(e)

        @block.gpsimd
        def _(e):
            po.run(e)


def constants():
    p = np.arange(128)
    c = np.zeros((128, CK), np.float32)

    def put(name, a):
        c[:, CW[name][0]:CW[name][1]] = a
    put("ident", np.eye(128, dtype=np.float32))
    i = 2 * p[:, None, None, None] + np.arange(2)[None, :, None, None]
    j = 2 * p[None, None, None, :] + np.arange(2)[None, None, :, None]
    put("dist", (np.clip(np.abs(i - j), 0, 10).astype(np.float32) * np.float32(0.01)).reshape(128, 512))
    put("upper", (p[:, None] < p[None, :]).astype(np.float32))
    put("e8", np.repeat(np.arange(8) - 8, 32).astype(np.float32)[None, :])
    put("unit", (128 * np.arange(72)).astype(np.float32)[None, :])
    put("head", (p[:, None] // 8 == np.arange(16)[None, :]).astype(np.float32))
    t = np.arange(NT)
    slot0 = ((t[None, :] // 2 * 128 + p[:, None]) * 4 + 2 * (t[None, :] % 2)).astype(np.int32)
    return c, np.concatenate([slot0, slot0 + 1], axis=1).astype(np.int32)


def layout(a):
    def rep(v):
        return np.broadcast_to(v.reshape(1, -1), (128, v.size))

    def halves(m):
        return np.concatenate([m[0:128], m[128:256]], axis=1)

    consts, dest = constants()
    wa = np.concatenate([a["L0_attn_W"].T, a["L0_ffn_router_w"].T, rep(a["L0_ffn_routing_bias"]),
                         a["L0_attn_b"].reshape(128, 1)], axis=1)
    wb = np.concatenate([a["L0_ffn_shared_gate"].T, a["L0_ffn_shared_up"].T, halves(a["L0_ffn_shared_down"].T)], axis=1)
    we = np.concatenate([np.concatenate([a["L0_ffn_gate_w"][e], a["L0_ffn_up_w"][e], halves(a["L0_ffn_down_w"][e])], axis=1)
                         for e in range(8)], axis=1)
    temp = a["L1_attn_temp"].reshape(16)
    wd = np.concatenate([a["L1_attn_Wqkv"].T, a["L1_attn_Wout"].T, a["L1_ffn_Wp1"], a["L1_ffn_Wp2"],
                         a["L1_ffn_bp1"].reshape(128, 1), rep(a["L1_ffn_bp2"]), rep(temp), rep(a["L1_attn_bout"]),
                         a["L1_ffn_Wo"], rep(a["L1_ffn_bo"])], axis=1)
    w1 = np.stack([np.concatenate([a["L1_ffn_W1"][e], halves(a["L1_ffn_W2"][e]), a["L1_ffn_b1"][e].reshape(2, 128).T,
                                   a["L1_ffn_b2"][e].reshape(128, 1), np.zeros((128, 1), np.float32)], axis=1)
                   for e in range(8)])
    return {"x": a["L0_attn_x"], "consts": consts, "dest": dest, "wa": wa, "wb": wb, "we": we, "wd": wd, "w1": w1}


def kernel(**inputs):
    import concourse.bacc as bacc
    from concourse.bass_utils import run_bass_kernel_spmd as run

    nc = bacc.Bacc("TRN2", target_bir_lowering=False, num_devices=1)
    arrays = {n: np.ascontiguousarray(v) for n, v in layout({k: np.asarray(v) for k, v in inputs.items()}).items()}
    aps = {n: nc.dram_tensor(f"in_{n}", v.shape, mybir.dt.from_np(v.dtype), kind="ExternalInput").ap()
           for n, v in arrays.items()}
    out = nc.dram_tensor("out_0", (16, 256, 128), F32, kind="ExternalOutput").ap()
    program(nc, aps, out)
    r = run(nc, [{f"in_{n}": v for n, v in arrays.items()}], core_ids=[0])
    return r.results[0]["out_0"]
```
